# Optimizing a Trainium2 kernel written in Bass

```python
import numpy as np
import jax
import jax.numpy as jnp

def _softmax(x, axis=-1):
    return jax.nn.softmax(x, axis=axis)

def _gelu(x):
    return jax.nn.gelu(x, approximate=True)

def _silu(x):
    return jax.nn.silu(x)

def _sigmoid(x):
    return jax.nn.sigmoid(x)

def _layernorm(x, axis=-1, eps=1e-05):
    m = jnp.mean(x, axis=axis, keepdims=True)
    v = jnp.var(x, axis=axis, keepdims=True)
    return (x - m) / jnp.sqrt(v + eps)

def _scatter_add(tgt, idx, src, axis=0):
    return tgt.at[idx].add(src)

def _segment_sum(src, seg, n):
    return jax.ops.segment_sum(src, seg, n)
kernel_name = 'mk_dlrm_tower_d1_rec_r8_92f896'

def setup_inputs(seed: int=0):
    np.random.seed(seed)
    _w = jnp.asarray

    def _rec_inputs():
        import jax
        import jax.numpy as jnp
        _tk = jax.random.key(seed)
        dense_ctx = jax.random.normal(jax.random.fold_in(_tk, 190), (512, 16), jnp.float32)
        ids = jnp.stack([jax.random.randint(jax.random.fold_in(_tk, 200 + f), (512,), 0, v, jnp.int32) for f, v in enumerate([125000, 1000, 1000, 125000, 125000, 1000, 1250, 125000, 12500, 125000, 125000, 125000, 125000, 1000, 125000, 1250, 1250, 1250, 1000, 125000, 12500, 1250, 1250, 125000, 12500, 12500, 1250, 1250, 1250, 12500, 1250, 1000, 1000, 1250, 125000, 125000, 1000, 12500, 1250])], axis=1)
        tbl_0 = 0.05 * jax.random.normal(jax.random.fold_in(_tk, 500 + 0), (125000, 16), jnp.float32)
        tbl_1 = 0.05 * jax.random.normal(jax.random.fold_in(_tk, 500 + 1), (1000, 16), jnp.float32)
        tbl_2 = 0.05 * jax.random.normal(jax.random.fold_in(_tk, 500 + 2), (1000, 16), jnp.float32)
        tbl_3 = 0.05 * jax.random.normal(jax.random.fold_in(_tk, 500 + 3), (125000, 16), jnp.float32)
        tbl_4 = 0.05 * jax.random.normal(jax.random.fold_in(_tk, 500 + 4), (125000, 16), jnp.float32)
        tbl_5 = 0.05 * jax.random.normal(jax.random.fold_in(_tk, 500 + 5), (1000, 16), jnp.float32)
        tbl_6 = 0.05 * jax.random.normal(jax.random.fold_in(_tk, 500 + 6), (1250, 16), jnp.float32)
        tbl_7 = 0.05 * jax.random.normal(jax.random.fold_in(_tk, 500 + 7), (125000, 16), jnp.float32)
        tbl_8 = 0.05 * jax.random.normal(jax.random.fold_in(_tk, 500 + 8), (12500, 16), jnp.float32)
        tbl_9 = 0.05 * jax.random.normal(jax.random.fold_in(_tk, 500 + 9), (125000, 16), jnp.float32)
        tbl_10 = 0.05 * jax.random.normal(jax.random.fold_in(_tk, 500 + 10), (125000, 16), jnp.float32)
        tbl_11 = 0.05 * jax.random.normal(jax.random.fold_in(_tk, 500 + 11), (125000, 16), jnp.float32)
        tbl_12 = 0.05 * jax.random.normal(jax.random.fold_in(_tk, 500 + 12), (125000, 16), jnp.float32)
        tbl_13 = 0.05 * jax.random.normal(jax.random.fold_in(_tk, 500 + 13), (1000, 16), jnp.float32)
        tbl_14 = 0.05 * jax.random.normal(jax.random.fold_in(_tk, 500 + 14), (125000, 16), jnp.float32)
        tbl_15 = 0.05 * jax.random.normal(jax.random.fold_in(_tk, 500 + 15), (1250, 16), jnp.float32)
        tbl_16 = 0.05 * jax.random.normal(jax.random.fold_in(_tk, 500 + 16), (1250, 16), jnp.float32)
        tbl_17 = 0.05 * jax.random.normal(jax.random.fold_in(_tk, 500 + 17), (1250, 16), jnp.float32)
        tbl_18 = 0.05 * jax.random.normal(jax.random.fold_in(_tk, 500 + 18), (1000, 16), jnp.float32)
        tbl_19 = 0.05 * jax.random.normal(jax.random.fold_in(_tk, 500 + 19), (125000, 16), jnp.float32)
        tbl_20 = 0.05 * jax.random.normal(jax.random.fold_in(_tk, 500 + 20), (12500, 16), jnp.float32)
        tbl_21 = 0.05 * jax.random.normal(jax.random.fold_in(_tk, 500 + 21), (1250, 16), jnp.float32)
        tbl_22 = 0.05 * jax.random.normal(jax.random.fold_in(_tk, 500 + 22), (1250, 16), jnp.float32)
        tbl_23 = 0.05 * jax.random.normal(jax.random.fold_in(_tk, 500 + 23), (125000, 16), jnp.float32)
        tbl_24 = 0.05 * jax.random.normal(jax.random.fold_in(_tk, 500 + 24), (12500, 16), jnp.float32)
        tbl_25 = 0.05 * jax.random.normal(jax.random.fold_in(_tk, 500 + 25), (12500, 16), jnp.float32)
        tbl_26 = 0.05 * jax.random.normal(jax.random.fold_in(_tk, 500 + 26), (1250, 16), jnp.float32)
        tbl_27 = 0.05 * jax.random.normal(jax.random.fold_in(_tk, 500 + 27), (1250, 16), jnp.float32)
        tbl_28 = 0.05 * jax.random.normal(jax.random.fold_in(_tk, 500 + 28), (1250, 16), jnp.float32)
        tbl_29 = 0.05 * jax.random.normal(jax.random.fold_in(_tk, 500 + 29), (12500, 16), jnp.float32)
        tbl_30 = 0.05 * jax.random.normal(jax.random.fold_in(_tk, 500 + 30), (1250, 16), jnp.float32)
        tbl_31 = 0.05 * jax.random.normal(jax.random.fold_in(_tk, 500 + 31), (1000, 16), jnp.float32)
        tbl_32 = 0.05 * jax.random.normal(jax.random.fold_in(_tk, 500 + 32), (1000, 16), jnp.float32)
        tbl_33 = 0.05 * jax.random.normal(jax.random.fold_in(_tk, 500 + 33), (1250, 16), jnp.float32)
        tbl_34 = 0.05 * jax.random.normal(jax.random.fold_in(_tk, 500 + 34), (125000, 16), jnp.float32)
        tbl_35 = 0.05 * jax.random.normal(jax.random.fold_in(_tk, 500 + 35), (125000, 16), jnp.float32)
        tbl_36 = 0.05 * jax.random.normal(jax.random.fold_in(_tk, 500 + 36), (1000, 16), jnp.float32)
        tbl_37 = 0.05 * jax.random.normal(jax.random.fold_in(_tk, 500 + 37), (12500, 16), jnp.float32)
        tbl_38 = 0.05 * jax.random.normal(jax.random.fold_in(_tk, 500 + 38), (1250, 16), jnp.float32)
        _rk = jax.random.fold_in(_tk, 7)
        W_top1 = 0.0606339 * jax.random.normal(jax.random.fold_in(_tk, 801), (272, 512), jnp.float32)
        W_top2 = 0.0441942 * jax.random.normal(jax.random.fold_in(_tk, 802), (512, 256), jnp.float32)
        W_top3 = 0.0625 * jax.random.normal(jax.random.fold_in(_tk, 803), (256, 1), jnp.float32)
        b_top1 = jnp.zeros((512,), jnp.float32)
        b_top2 = jnp.zeros((256,), jnp.float32)
        return (dense_ctx, ids, tbl_0, tbl_1, tbl_2, tbl_3, tbl_4, tbl_5, tbl_6, tbl_7, tbl_8, tbl_9, tbl_10, tbl_11, tbl_12, tbl_13, tbl_14, tbl_15, tbl_16, tbl_17, tbl_18, tbl_19, tbl_20, tbl_21, tbl_22, tbl_23, tbl_24, tbl_25, tbl_26, tbl_27, tbl_28, tbl_29, tbl_30, tbl_31, tbl_32, tbl_33, tbl_34, tbl_35, tbl_36, tbl_37, tbl_38, W_top1, b_top1, W_top2, b_top2, W_top3)
    dense_ctx, ids, tbl_0, tbl_1, tbl_2, tbl_3, tbl_4, tbl_5, tbl_6, tbl_7, tbl_8, tbl_9, tbl_10, tbl_11, tbl_12, tbl_13, tbl_14, tbl_15, tbl_16, tbl_17, tbl_18, tbl_19, tbl_20, tbl_21, tbl_22, tbl_23, tbl_24, tbl_25, tbl_26, tbl_27, tbl_28, tbl_29, tbl_30, tbl_31, tbl_32, tbl_33, tbl_34, tbl_35, tbl_36, tbl_37, tbl_38, W_top1, b_top1, W_top2, b_top2, W_top3 = _rec_inputs()

    def _L0_rec_setup():
        import jax, jax.numpy as jnp
        import numpy as np
        B, M, D = (1024, 39, 16)
        S1, S2 = (128, 128)

        def _cin_layer(x0, xk, W, b):
            out = jnp.einsum('bhd,bmd,shm->bsd', xk, x0, W) + b[None, :, None]
            return jax.nn.relu(out)
        key = jax.random.key(seed)
        k0, k1, k2 = jax.random.split(key, 3)
        x0 = jax.random.normal(k0, (B, M, D), dtype=jnp.float32)
        W1 = jax.random.normal(k1, (S1, M, M), dtype=jnp.float32) * 0.05
        b1 = jnp.zeros((S1,), dtype=jnp.float32)
        W2 = jax.random.normal(k2, (S2, S1, M), dtype=jnp.float32) * 0.05
        b2 = jnp.zeros((S2,), dtype=jnp.float32)
        return {'x0': x0, 'W1': W1, 'b1': b1, 'W2': W2, 'b2': b2}
    _L0_rec_all = _L0_rec_setup()
    _L0_rec_in = {k: v for k, v in _L0_rec_all.items() if k in ('W1', 'b1', 'W2', 'b2')}
    del _L0_rec_all
    return {'dense_ctx': dense_ctx, 'ids': ids, 'tbl_0': tbl_0, 'tbl_1': tbl_1, 'tbl_2': tbl_2, 'tbl_3': tbl_3, 'tbl_4': tbl_4, 'tbl_5': tbl_5, 'tbl_6': tbl_6, 'tbl_7': tbl_7, 'tbl_8': tbl_8, 'tbl_9': tbl_9, 'tbl_10': tbl_10, 'tbl_11': tbl_11, 'tbl_12': tbl_12, 'tbl_13': tbl_13, 'tbl_14': tbl_14, 'tbl_15': tbl_15, 'tbl_16': tbl_16, 'tbl_17': tbl_17, 'tbl_18': tbl_18, 'tbl_19': tbl_19, 'tbl_20': tbl_20, 'tbl_21': tbl_21, 'tbl_22': tbl_22, 'tbl_23': tbl_23, 'tbl_24': tbl_24, 'tbl_25': tbl_25, 'tbl_26': tbl_26, 'tbl_27': tbl_27, 'tbl_28': tbl_28, 'tbl_29': tbl_29, 'tbl_30': tbl_30, 'tbl_31': tbl_31, 'tbl_32': tbl_32, 'tbl_33': tbl_33, 'tbl_34': tbl_34, 'tbl_35': tbl_35, 'tbl_36': tbl_36, 'tbl_37': tbl_37, 'tbl_38': tbl_38, 'W_top1': W_top1, 'b_top1': b_top1, 'W_top2': W_top2, 'b_top2': b_top2, 'W_top3': W_top3, 'L0_rec_W1': _L0_rec_in['W1'], 'L0_rec_b1': _L0_rec_in['b1'], 'L0_rec_W2': _L0_rec_in['W2'], 'L0_rec_b2': _L0_rec_in['b2']}

def reference(dense_ctx, ids, tbl_0, tbl_1, tbl_2, tbl_3, tbl_4, tbl_5, tbl_6, tbl_7, tbl_8, tbl_9, tbl_10, tbl_11, tbl_12, tbl_13, tbl_14, tbl_15, tbl_16, tbl_17, tbl_18, tbl_19, tbl_20, tbl_21, tbl_22, tbl_23, tbl_24, tbl_25, tbl_26, tbl_27, tbl_28, tbl_29, tbl_30, tbl_31, tbl_32, tbl_33, tbl_34, tbl_35, tbl_36, tbl_37, tbl_38, W_top1, b_top1, W_top2, b_top2, W_top3, L0_rec_W1, L0_rec_b1, L0_rec_W2, L0_rec_b2):
    import jax
    import jax.numpy as jnp

    def _L0_rec_ref(x0, W1, b1, W2, b2):
        import jax, jax.numpy as jnp
        import numpy as np
        B, M, D = (1024, 39, 16)
        S1, S2 = (128, 128)

        def _cin_layer(x0, xk, W, b):
            out = jnp.einsum('bhd,bmd,shm->bsd', xk, x0, W) + b[None, :, None]
            return jax.nn.relu(out)
        x1 = _cin_layer(x0, x0, W1, b1)
        x2 = _cin_layer(x0, x1, W2, b2)
        p1 = x1.sum(axis=-1)
        p2 = x2.sum(axis=-1)
        return jnp.concatenate([p1, p2], axis=-1)
    e = jnp.stack([tbl_0[ids[:, 0]], tbl_1[ids[:, 1]], tbl_2[ids[:, 2]], tbl_3[ids[:, 3]], tbl_4[ids[:, 4]], tbl_5[ids[:, 5]], tbl_6[ids[:, 6]], tbl_7[ids[:, 7]], tbl_8[ids[:, 8]], tbl_9[ids[:, 9]], tbl_10[ids[:, 10]], tbl_11[ids[:, 11]], tbl_12[ids[:, 12]], tbl_13[ids[:, 13]], tbl_14[ids[:, 14]], tbl_15[ids[:, 15]], tbl_16[ids[:, 16]], tbl_17[ids[:, 17]], tbl_18[ids[:, 18]], tbl_19[ids[:, 19]], tbl_20[ids[:, 20]], tbl_21[ids[:, 21]], tbl_22[ids[:, 22]], tbl_23[ids[:, 23]], tbl_24[ids[:, 24]], tbl_25[ids[:, 25]], tbl_26[ids[:, 26]], tbl_27[ids[:, 27]], tbl_28[ids[:, 28]], tbl_29[ids[:, 29]], tbl_30[ids[:, 30]], tbl_31[ids[:, 31]], tbl_32[ids[:, 32]], tbl_33[ids[:, 33]], tbl_34[ids[:, 34]], tbl_35[ids[:, 35]], tbl_36[ids[:, 36]], tbl_37[ids[:, 37]], tbl_38[ids[:, 38]]], axis=1)
    z = _L0_rec_ref(e, L0_rec_W1, L0_rec_b1, L0_rec_W2, L0_rec_b2)
    z = z.reshape(z.shape[0], -1)
    h = jnp.concatenate([z, dense_ctx], axis=1)
    h = jnp.maximum(h @ W_top1 + b_top1, 0.0)
    h = jnp.maximum(h @ W_top2 + b_top2, 0.0)
    y = h @ W_top3
    return y

_drawn_inputs = setup_inputs


def setup_inputs(seed=0):
    import zlib

    import numpy as np

    out = dict(_drawn_inputs(seed))
    spreads = {'b_top1': (0.0, 0.1),
     'b_top2': (0.0, 0.1),
     'L0_rec_b1': (0.0, 0.1),
     'L0_rec_b2': (0.0, 0.1)}
    factors = {'tbl_0': 4.729,
     'tbl_1': 4.423,
     'tbl_2': 7.457,
     'tbl_3': 6.508,
     'tbl_4': 6.877,
     'tbl_5': 7.471,
     'tbl_6': 6.003,
     'tbl_7': 4.398,
     'tbl_8': 8.0,
     'tbl_9': 6.985,
     'tbl_10': 6.494,
     'tbl_11': 5.945,
     'tbl_12': 5.408,
     'tbl_14': 7.861,
     'tbl_15': 6.893,
     'tbl_16': 7.473,
     'tbl_17': 4.815,
     'tbl_18': 5.778,
     'tbl_19': 4.729,
     'tbl_20': 8.0,
     'tbl_21': 3.369,
     'tbl_22': 8.0,
     'tbl_23': 7.402,
     'tbl_24': 7.974,
     'tbl_25': 4.976,
     'tbl_26': 4.288,
     'tbl_27': 6.684,
     'tbl_28': 7.872,
     'tbl_29': 5.503,
     'tbl_30': 5.477,
     'tbl_31': 3.158,
     'tbl_32': 8.0,
     'tbl_33': 8.0,
     'tbl_34': 7.43,
     'tbl_35': 7.76,
     'tbl_36': 8.0,
     'tbl_37': 8.0,
     'tbl_38': 6.438,
     'tbl_13': 4.06}
    for name, (base, spread) in spreads.items():
        noise = np.random.default_rng([zlib.crc32(name.encode()), seed]).standard_normal(out[name].shape)
        drawn = base * np.exp(spread * noise) if base else spread * noise
        out[name] = jnp.asarray(drawn.astype(out[name].dtype))
    for name, factor in factors.items():
        out[name] = (out[name] * factor).astype(out[name].dtype)
    return out
```

```python
from contextlib import ExitStack

import concourse.bass as bass
from concourse import mybir

F32 = mybir.dt.float32
F32R = mybir.dt.float32r
BF16 = mybir.dt.bfloat16
I32 = mybir.dt.int32
ALU = mybir.AluOpType
ACT = mybir.ActivationFunctionType
AX = mybir.AxisListType

P = 128
M = 39
D = 16
S = 128
PARTS = 3
STACK = 3
ROWS = STACK * M
SHIFTS = (M + 1) // 2
PAIR_TILES = -(-SHIFTS // STACK)
LAST_ROWS = (SHIFTS - STACK * (PAIR_TILES - 1)) * M
CD = 4
CW = CD * P
FIELDS_IN_BANK = 4
BANKS = -(-M // FIELDS_IN_BANK)
SHORT = BANKS * FIELDS_IN_BANK - M
SLOTS = CD * BANKS
RING = 4
HALF = BANKS // 2
ACCS = SLOTS // 2 * FIELDS_IN_BANK

TURN_AT = 0
STACK_AT = 3
ROT_AT = [5 + 4 * t for t in range(PAIR_TILES)]
PAIR_AT = [9 + 4 * t for t in range(PAIR_TILES)]
TURN_COPY_AT = 3
STACK_COPY_AT = 5
PRODUCT_AT = [8 + 4 * t for t in range(PAIR_TILES)]
X1_COPY_AT = 37
X1_SPLIT_AT = 38
FOLD_AT = 6


def fields_of(slot):
    width = FIELDS_IN_BANK - SHORT if slot == 1 else FIELDS_IN_BANK
    first = FIELDS_IN_BANK * slot - (SHORT if slot > 1 else 0)
    return first, width


def after(engine, semaphore, value):
    if isinstance(value, int) and value <= 0:
        return
    engine.wait_ge(semaphore, value)


def build(nc, ids, tables, ctx_t, w1_a, w1_b, b1, w2_t, b2, select, ident,
          w_top1, b_top1, w_top2, b_top2, w_top3, out):
    B = ids.shape[0]
    TILES = B // P
    CHUNKS_IN_TILE = D // CD
    CHUNKS = TILES * CHUNKS_IN_TILE
    PAIRS = CHUNKS // 2
    N1, N2 = w_top1.shape[1], w_top2.shape[1]
    T1, T2 = N1 // P, N2 // P
    CTX = ctx_t.shape[0]

    with ExitStack() as ctx:
        def sb(name, shape, dt=F32):
            return ctx.enter_context(nc.sbuf_tensor(name, shape, dt))

        def psum(name, shape, dt=F32):
            return ctx.enter_context(nc.psum_tensor(name, shape, dt))

        def sem(name):
            return ctx.enter_context(nc.semaphore(name))

        idx_all = sb("idx_all", [P, TILES, M], I32)
        select_f = sb("select_f", [ROWS, (PAIR_TILES + 1) * ROWS])
        select_b = sb("select_b", [ROWS, PAIR_TILES + 1, ROWS], BF16)
        ident_f = sb("ident_f", [P, P])
        ident_b = sb("ident_b", [P, P], BF16)
        w1_sym = sb("w1_sym", [ROWS, PAIR_TILES, S])
        w1_other = sb("w1_other", [ROWS, PAIR_TILES, S])
        w2_f = sb("w2_f", [S, M * S])
        w2_hi = sb("w2_hi", [S, M * S], F32R)
        w2_lo = sb("w2_lo", [S, M * S], F32R)
        b1_col = sb("b1_col", [S, 1])
        b2_rows = sb("b2_rows", [P, S])
        wt1 = sb("wt1", [P, 2, N1])
        wt1_ctx = sb("wt1_ctx", [CTX, N1])
        wt2 = sb("wt2", [P, T1, N2])
        wt3 = sb("wt3", [P, T2])
        bt1 = sb("bt1", [P, T1])
        bt2 = sb("bt2", [P, T2])
        ctx_sb = sb("ctx_sb", [CTX, B])
        gathered = sb("gathered", [P, M, D])
        x0_all = sb("x0_all", [P, TILES * D, M])
        parts_all = sb("parts_all", [P, TILES * D, PARTS, M], BF16)
        rest = sb("rest", [P, 2, D, M])
        x0_chunk = [sb(f"x0_chunk{i}", [P, CD, M]) for i in range(2)]
        parts_t = sb("parts_t", [ROWS, CW], BF16)
        plain = sb("plain", [ROWS, CW])
        product = [sb(f"product{i}", [ROWS, CW]) for i in range(2)]
        x1 = sb("x1", [S, CW])
        x1_hi = [sb(f"x1_hi{i}", [S, CW], F32R) for i in range(2)]
        x1_lo = [sb(f"x1_lo{i}", [S, CW], F32R) for i in range(2)]
        prods = [sb(f"prods{i}", [P, HALF, FIELDS_IN_BANK * S]) for i in range(2)]
        pool_sum = sb("pool_sum", [P, 2, FIELDS_IN_BANK * S])
        sums = [sb(f"sums{i}", [P, 2 + FIELDS_IN_BANK, S]) for i in range(2)]
        x2 = sb("x2", [P, 2, S])
        p1_chunk = sb("p1_chunk", [S, CHUNKS * P])
        p2_chunk = sb("p2_chunk", [P, CHUNKS * S])
        p1_t = sb("p1_t", [S, B])
        p2 = sb("p2", [P, TILES, S])
        p2_t = sb("p2_t", [S, B])
        h1 = sb("h1", [P, T1, B])
        h2 = sb("h2", [P, T2, B])
        y_row = sb("y_row", [1, B])

        y_bank = [psum(f"y_bank{i}", [P, FIELDS_IN_BANK * S]) for i in range(RING)]
        rot_bank = [psum(f"rot_bank{i}", [P, CW]) for i in range(2)]
        turn_bank = psum("turn_bank", [P, CW])
        x1_bank = psum("x1_bank", [P, CW])
        mlp_bank = [turn_bank, x1_bank, *rot_bank]

        ids_in = sem("ids_in")
        w1_in = sem("w1_in")
        const_in = sem("const_in")
        w2_in = sem("w2_in")
        b2_in = sem("b2_in")
        top_in = sem("top_in")
        rows_in = sem("rows_in")
        out_sent = sem("out_sent")
        const_done = sem("const_done")
        w1_zeroed = sem("w1_zeroed")
        w1_done = sem("w1_done")
        w2_hi_done = sem("w2_hi_done")
        w2_lo_done = sem("w2_lo_done")
        split_step = sem("split_step")
        parts_done = sem("parts_done")
        x0_done = sem("x0_done")
        turned = sem("turned")
        turn_copied = sem("turn_copied")
        rotated = sem("rotated")
        plain_done = sem("plain_done")
        product_done = sem("product_done")
        pairs_done = sem("pairs_done")
        x1_done = sem("x1_done")
        x1_used = sem("x1_used")
        y_even = sem("y_even")
        y_odd = sem("y_odd")
        acc_done = sem("acc_done")
        prods_done = sem("prods_done")
        pool_step = sem("pool_step")
        fold_step = sem("fold_step")
        p1_done = sem("p1_done")
        p2_done = sem("p2_done")
        p2_turned = sem("p2_turned")
        p2_t_done = sem("p2_t_done")
        h1_full = sem("h1_full")
        h1_done = sem("h1_done")
        h2_full = sem("h2_full")
        h2_done = sem("h2_done")
        y_full = sem("y_full")
        y_done = sem("y_done")

        POOL_STEPS = 4
        LAST_POOL = POOL_STEPS
        SPLIT_STEPS = 6

        def chunk_pairs(engine, chunk):
            for half in range(2):
                chunk(half, half)
            with engine.Fori(1, PAIRS - 1) as pair:
                for half in range(2):
                    chunk(pair * 2 + half, half)
            for half in range(2):
                chunk(CHUNKS - 2 + half, half)

        def has_next(c):
            return not (isinstance(c, int) and c == CHUNKS - 1)

        block = ctx.enter_context(nc.Block())

        @block.sync
        def _(sp):
            sp.dma_start(idx_all[:], ids.rearrange("(t p) f -> p t f", p=P)).then_inc(ids_in, 16)
            sp.dma_start(select_f[:], select).then_inc(const_in, 16)
            sp.dma_start(ident_f[:], ident).then_inc(const_in, 16)
            sp.dma_start(w1_sym[:], w1_a).then_inc(w1_in, 16)
            sp.dma_start(w1_other[:], w1_b).then_inc(w1_in, 16)
            sp.dma_start(b1_col[:], b1.rearrange("(s a) -> s a", a=1)).then_inc(w1_in, 16)
            sp.dma_start(w2_f[:], w2_t).then_inc(w2_in, 16)
            sp.dma_start(b2_rows[:], b2.rearrange("(a s) -> a s", a=1).broadcast_to([P, S])).then_inc(b2_in, 16)
            sp.dma_start(wt1[:], w_top1[0:2 * P, :].rearrange("(t p) n -> p t n", p=P)).then_inc(top_in, 16)
            sp.dma_start(wt1_ctx[:], w_top1[2 * P:2 * P + CTX, :]).then_inc(top_in, 16)
            sp.dma_start(wt2[:], w_top2.rearrange("(t p) n -> p t n", p=P)).then_inc(top_in, 16)
            sp.dma_start(wt3[:], w_top3).then_inc(top_in, 16)
            sp.dma_start(bt1[:], b_top1).then_inc(top_in, 16)
            sp.dma_start(bt2[:], b_top2).then_inc(top_in, 16)
            sp.dma_start(ctx_sb[:], ctx_t).then_inc(top_in, 16)
            sp.wait_ge(y_done, 1)
            sp.dma_start(out.rearrange("b a -> a b"), y_row[:]).then_inc(out_sent, 16)
            sp.wait_ge(out_sent, 16)
        TOP_DMAS = 7

        @block.gpsimd
        def _(pool):
            def gather(tile, field):
                if field == 0:
                    after(pool, split_step, tile * SPLIT_STEPS)
                nc.gpsimd.indirect_dma_start(
                    out=gathered[:, field, :], out_offset=None, in_=tables[field],
                    in_offset=bass.IndirectOffsetOnAxis(ap=idx_all[:, tile, field:field + 1], axis=0),
                ).then_inc(rows_in, 16)

            def split(tile):
                own = x0_all[:, bass.ds(tile * D, D), :]
                part = [parts_all[:, bass.ds(tile * D, D), i, :] for i in range(PARTS)]
                done = tile * SPLIT_STEPS
                pool.wait_ge(rows_in, (tile + 1) * (16 * M))
                nc.gpsimd.tensor_copy(own, gathered[:].rearrange("p f d -> p d f")).then_inc(split_step, 1)
                pool.wait_ge(split_step, done + 1)
                nc.gpsimd.tensor_copy(part[0], own).then_inc(split_step, 1)
                pool.wait_ge(split_step, done + 2)
                nc.gpsimd.tensor_tensor(rest[:, 0], own, part[0], ALU.subtract).then_inc(split_step, 1)
                pool.wait_ge(split_step, done + 3)
                nc.gpsimd.tensor_copy(part[1], rest[:, 0]).then_inc(split_step, 1)
                pool.wait_ge(split_step, done + 4)
                nc.gpsimd.tensor_tensor(rest[:, 1], rest[:, 0], part[1], ALU.subtract).then_inc(split_step, 1)
                pool.wait_ge(split_step, done + 5)
                nc.gpsimd.tensor_copy(part[2], rest[:, 1]).then_inc(split_step, 1)
                pool.wait_ge(split_step, done + 6)
                pool.engine_nop().then_inc(parts_done, CHUNKS_IN_TILE)

            def sum_products(n, k):
                bank = prods[k % 2]
                full = FIELDS_IN_BANK * S
                short = (FIELDS_IN_BANK - SHORT) * S
                total = sums[k % 2][:, 2:, :].rearrange("p a s -> p (a s)")
                step = n * POOL_STEPS
                pool.wait_ge(prods_done, n * HALF + 3)
                nc.gpsimd.tensor_tensor(pool_sum[:, 0], bank[:, 1], bank[:, 2], ALU.add).then_inc(pool_step, 1)
                pool.wait_ge(prods_done, n * HALF + 4)
                nc.gpsimd.tensor_tensor(bank[:, 3, 0:short], bank[:, 3, 0:short], bank[:, 0, 0:short],
                                        ALU.add).then_inc(pool_step, 1)
                pool.wait_ge(pool_step, step + 2)
                nc.gpsimd.tensor_tensor(pool_sum[:, 1], pool_sum[:, 0], bank[:, 3], ALU.add).then_inc(pool_step, 1)
                pool.wait_ge(prods_done, n * HALF + 5)
                pool.wait_ge(pool_step, step + 3)
                after(pool, fold_step, n * 2 - 3)
                nc.gpsimd.tensor_tensor(total[:, 0:full], pool_sum[:, 1], bank[:, 4], ALU.add).then_inc(pool_step, 1)

            def sample_tile(tile, fetch_next):
                field = 0
                for q in range(CHUNKS_IN_TILE):
                    for k in range(CD):
                        if fetch_next and q < 3:
                            upto = min(M, -(-M * (q * CD + k + 1) // (11)))
                            for field in range(field, upto):
                                gather(tile + 1, field)
                            field = upto
                            if q == 2 and k == 3:
                                split(tile + 1)
                        sum_products(tile * D + (q * CD + k), k)

            pool.wait_ge(ids_in, 16)
            for field in range(M):
                gather(0, field)
            split(0)
            for tile in range(TILES):
                sample_tile(tile, tile + 1 < TILES)

        @block.tensor
        def _(pe):
            def turn(c):
                pe.wait_ge(parts_done, c + 1)
                after(pe, turn_copied, c)
                for k in range(CD):
                    last = nc.tensor.matmul(
                        turn_bank[0:ROWS, k * P:(k + 1) * P],
                        parts_all[:, bass.ds(c * CD + k, 1), :, :].rearrange("p a i f -> p (a i f)"),
                        ident_b[:], start=True, stop=True)
                last.then_inc(turned, 1)

            def rotate(c, v):
                if v == 0:
                    pe.wait_ge(turn_copied, c + 1)
                if v == 2:
                    pe.wait_ge(plain_done, c + 1)
                else:
                    after(pe, product_done, c * PAIR_TILES + (v - 1 if v < 2 else v - 2))
                nc.tensor.matmul(rot_bank[v % 2][0:ROWS, :], select_b[:, v, :], parts_t[:],
                                 start=True, stop=True).then_inc(rotated, 1)

            def contract_pairs(c, t):
                if t == 0:
                    after(pe, x1_done, c * 2)
                pe.wait_ge(product_done, c * PAIR_TILES + (t + 1))
                rows = LAST_ROWS if t == PAIR_TILES - 1 else ROWS
                z = product[t % 2]
                nc.tensor.matmul(x1_bank[:], w1_sym[0:rows, t, :], z[0:rows, :],
                                 start=(t == 0), stop=(t == PAIR_TILES - 1)).then_inc(pairs_done, 1)

            def chunk(c, half):
                pe.wait_ge(x1_done, c * 2 + 2)
                pe.wait_ge(x1_used, c * 2 + 1)
                for slot in range(SLOTS):
                    if has_next(c):
                        if slot == TURN_AT:
                            turn(c + 1)
                        if slot == STACK_AT:
                            rotate(c + 1, 0)
                        if slot in ROT_AT:
                            rotate(c + 1, ROT_AT.index(slot) + 1)
                        if slot in PAIR_AT:
                            contract_pairs(c + 1, PAIR_AT.index(slot))
                    k, j = slot // BANKS, slot // 2
                    first, width = fields_of(slot % BANKS)
                    cols = slice(first * S, (first + width) * S)
                    hi = x1_hi[half][:, k * P:(k + 1) * P]
                    lo = x1_lo[half][:, k * P:(k + 1) * P]
                    y = y_bank[slot % RING][:, 0:width * S]
                    if slot % 2 == 0:
                        after(pe, acc_done, c * ACCS + (j - 1) * FIELDS_IN_BANK)
                    else:
                        after(pe, prods_done, c * (SLOTS // 2) + (j - 1))
                    nc.tensor.matmul(y, hi, w2_hi[:, cols], start=True, stop=False)
                    nc.tensor.matmul(y, hi, w2_lo[:, cols], start=False, stop=False)
                    nc.tensor.matmul(y, lo, w2_hi[:, cols], start=False, stop=True
                                     ).then_inc(y_even if slot % 2 == 0 else y_odd, 1)

            pe.wait_ge(const_done, 2)
            turn(0)
            rotate(0, 0)
            rotate(0, 1)
            pe.wait_ge(w1_done, 1)
            for t in range(PAIR_TILES):
                if t + 1 < PAIR_TILES:
                    rotate(0, t + 2)
                contract_pairs(0, t)
            pe.wait_ge(w2_hi_done, 1)
            pe.wait_ge(w2_lo_done, 1)
            chunk_pairs(pe, chunk)

            pe.wait_ge(top_in, 16 * TOP_DMAS)
            pe.wait_ge(p1_done, 1)
            for t in range(T1):
                cols = slice(t * P, (t + 1) * P)
                nc.tensor.matmul(mlp_bank[t][:], wt1[:, 0, cols], p1_t[:], start=True, stop=False)
                nc.tensor.matmul(mlp_bank[t][:], wt1_ctx[:, cols], ctx_sb[:], start=False, stop=False)
            pe.wait_ge(p2_done, 1)
            for b in range(TILES):
                last = nc.tensor.transpose(y_bank[0][:, b * P:(b + 1) * P], p2[:, b, :], ident_f[:])
            last.then_inc(p2_turned, 1)
            pe.wait_ge(p2_t_done, 1)
            for t in range(T1):
                nc.tensor.matmul(mlp_bank[t][:], wt1[:, 1, t * P:(t + 1) * P], p2_t[:],
                                 start=False, stop=True).then_inc(h1_full, 1)
            for t in range(T1):
                pe.wait_ge(h1_done, t + 1)
                for u in range(T2):
                    last = nc.tensor.matmul(y_bank[1 + u][:], wt2[:, t, u * P:(u + 1) * P], h1[:, t, :],
                                            start=(t == 0), stop=(t == T1 - 1))
                    if t == T1 - 1:
                        last.then_inc(h2_full, 1)
            for u in range(T2):
                pe.wait_ge(h2_done, u + 1)
                last = nc.tensor.matmul(y_bank[3][0:1, :], wt3[:, u:u + 1], h2[:, u, :],
                                        start=(u == 0), stop=(u == T2 - 1))
            last.then_inc(y_full, 1)

        @block.scalar
        def _(act):
            def scalars(c, half):
                act.wait_ge(parts_done, c + 1)
                after(act, acc_done, (c - 1) * ACCS)
                after(act, prods_done, (c - 1) * (SLOTS // 2))
                nc.scalar.activation(x0_chunk[half][:], x0_all[:, bass.ds(c * CD, CD), :],
                                     ACT.Copy).then_inc(x0_done, 1)

            def copy_turned(c):
                act.wait_ge(turned, c + 1)
                after(act, rotated, c * (PAIR_TILES + 1))
                nc.scalar.activation(parts_t[:], turn_bank[0:ROWS, :], ACT.Copy).then_inc(turn_copied, 1)

            def copy_plain(c):
                act.wait_ge(rotated, c * (PAIR_TILES + 1) + 1)
                after(act, product_done, c * PAIR_TILES)
                nc.scalar.activation(plain[:], rot_bank[0][0:ROWS, :], ACT.Copy).then_inc(plain_done, 1)

            def finish_x1(c, half):
                act.wait_ge(pairs_done, (c + 1) * PAIR_TILES)
                after(act, x1_used, c * 2)
                nc.scalar.activation(x1[:], x1_bank[:], ACT.Relu, bias=b1_col[:]).then_inc(x1_done, 1)
                nc.scalar.activation(x1_hi[half][:], x1_bank[:], ACT.Relu, bias=b1_col[:]).then_inc(x1_done, 1)

            def chunk(c, half):
                act.wait_ge(x0_done, c + 1)
                for slot in range(1, SLOTS, 2):
                    if has_next(c):
                        if slot == 1:
                            scalars(c + 1, 1 - half)
                        if slot == TURN_COPY_AT:
                            copy_turned(c + 1)
                        if slot == STACK_COPY_AT:
                            copy_plain(c + 1)
                        if slot == X1_COPY_AT:
                            finish_x1(c + 1, 1 - half)
                    k, j = slot // BANKS, slot // 2
                    first, width = fields_of(slot % BANKS)
                    act.wait_ge(y_odd, c * (SLOTS // 2) + (j + 1))
                    if slot % BANKS == 1:
                        after(act, pool_step, (c * CD + (k - 1)) * POOL_STEPS)
                    for f in range(width):
                        last = nc.scalar.activation(
                            prods[k % 2][:, j % HALF, f * S:(f + 1) * S],
                            y_bank[slot % RING][:, f * S:(f + 1) * S], ACT.Copy,
                            scale=x0_chunk[half][:, k, first + f:first + f + 1])
                    last.then_inc(prods_done, 1)

            act.wait_ge(const_in, 32)
            nc.scalar.activation(select_b[:].rearrange("p v r -> p (v r)"), select_f[:],
                                 ACT.Copy).then_inc(const_done, 1)
            nc.scalar.activation(ident_b[:], ident_f[:], ACT.Copy).then_inc(const_done, 1)
            act.wait_ge(w2_in, 16)
            nc.scalar.activation(w2_hi[:], w2_f[:], ACT.Copy).then_inc(w2_hi_done, 1)
            act.wait_ge(w1_in, 48)
            scalars(0, 0)
            copy_turned(0)
            copy_plain(0)
            finish_x1(0, 0)
            chunk_pairs(act, chunk)

            act.wait_ge(top_in, 16 * TOP_DMAS)
            for t in range(T1):
                act.wait_ge(h1_full, t + 1)
                nc.scalar.activation(h1[:, t, :], mlp_bank[t][:], ACT.Relu, bias=bt1[:, t:t + 1]).then_inc(h1_done, 1)
            for u in range(T2):
                act.wait_ge(h2_full, u + 1)
                nc.scalar.activation(h2[:, u, :], y_bank[1 + u][:], ACT.Relu, bias=bt2[:, u:u + 1]).then_inc(h2_done, 1)

        @block.vector
        def _(dve):
            def multiply_pairs(c, t):
                dve.wait_ge(rotated, c * (PAIR_TILES + 1) + (t + 2))
                dve.wait_ge(plain_done, c + 1)
                after(dve, pairs_done, c * PAIR_TILES + (t - 1 if t >= 2 else 0))
                nc.vector.tensor_tensor(product[t % 2][:], rot_bank[(t + 1) % 2][0:ROWS, :], plain[:],
                                        ALU.mult).then_inc(product_done, 1)

            def split_x1(c, half):
                dve.wait_ge(x1_done, c * 2 + 2)
                nc.vector.tensor_tensor(x1_lo[half][:], x1[:], x1_hi[half][:].bitcast(F32),
                                        ALU.subtract).then_inc(x1_used, 1)
                nc.vector.tensor_reduce(p1_chunk[:, bass.ds(c * P, P)], x1[:].rearrange("h (d b) -> h b d", d=CD),
                                        AX.X, ALU.add).then_inc(x1_used, 1)

            def fold(c, k):
                n = c * CD + k
                here = p2_chunk[:, bass.ds(c * S, S)]
                dve.wait_ge(pool_step, n * POOL_STEPS + LAST_POOL)
                dve.wait_ge(acc_done, c * ACCS + (k + 1) * HALF * FIELDS_IN_BANK)
                nc.vector.tensor_reduce(x2[:, k % 2, :], sums[k % 2][:].rearrange("p a s -> p s a"),
                                        AX.X, ALU.add).then_inc(fold_step, 1)
                dve.wait_ge(fold_step, n * 2 + 1)
                if k == 0:
                    nc.vector.tensor_scalar(here, x2[:, k % 2, :], 0.0, None, ALU.max).then_inc(fold_step, 1)
                else:
                    nc.vector.scalar_tensor_tensor(out=here, in0=x2[:, k % 2, :], scalar=0.0, in1=here,
                                                   op0=ALU.max, op1=ALU.add).then_inc(fold_step, 1)

            def chunk(c, half):
                dve.wait_ge(x0_done, c + 1)
                for slot in range(0, SLOTS, 2):
                    if has_next(c):
                        if slot in PRODUCT_AT:
                            multiply_pairs(c + 1, PRODUCT_AT.index(slot))
                        if slot == X1_SPLIT_AT:
                            split_x1(c + 1, 1 - half)
                    k, j = slot // BANKS, slot // 2
                    if slot % BANKS == FOLD_AT:
                        if k > 0:
                            fold(c, k - 1)
                        elif not (isinstance(c, int) and c == 0):
                            fold(c - 1, CD - 1)
                    first, width = fields_of(slot % BANKS)
                    dve.wait_ge(y_even, c * (SLOTS // 2) + (j + 1))
                    for f in range(width):
                        y = y_bank[slot % RING][:, f * S:(f + 1) * S]
                        x = x0_chunk[half][:, k, first + f:first + f + 1]
                        acc = sums[k % 2][:, f % 2, :]
                        after(dve, acc_done, c * ACCS + (j * FIELDS_IN_BANK + f - 1))
                        if slot % BANKS == 0 and f == 0:
                            after(dve, fold_step, (c * CD + k) * 2 - 3)
                        if slot % BANKS == 0 and f == 1:
                            nc.vector.tensor_scalar(acc, y, x, None, ALU.mult).then_inc(acc_done, 1)
                        else:
                            start = slot % BANKS == 0 and f == 0
                            nc.vector.scalar_tensor_tensor(out=acc, in0=y, scalar=x, in1=b2_rows[:] if start else acc,
                                                           op0=ALU.mult, op1=ALU.add).then_inc(acc_done, 1)

            dve.wait_ge(w1_in, 48)
            nc.vector.memset(w1_other[0:M, 0, :], 0.0).then_inc(w1_zeroed, 1)
            dve.wait_ge(w1_zeroed, 1)
            nc.vector.tensor_tensor(w1_sym[:], w1_sym[:], w1_other[:], ALU.add).then_inc(w1_done, 1)
            dve.wait_ge(w2_hi_done, 1)
            nc.vector.tensor_tensor(w2_lo[:], w2_f[:], w2_hi[:].bitcast(F32), ALU.subtract).then_inc(w2_lo_done, 1)
            for t in range(PAIR_TILES):
                multiply_pairs(0, t)
            split_x1(0, 0)
            dve.wait_ge(b2_in, 16)
            chunk_pairs(dve, chunk)

            dve.wait_ge(x1_used, CHUNKS * 2)
            nc.vector.tensor_reduce(p1_t[:].rearrange("h (t b) -> h t b", t=TILES),
                                    p1_chunk[:].rearrange("h (t q b) -> h t b q", t=TILES, b=P),
                                    AX.X, ALU.add).then_inc(p1_done, 1)
            fold(CHUNKS - 1, CD - 1)
            dve.wait_ge(fold_step, CHUNKS * CD * 2)
            nc.vector.tensor_reduce(p2[:], p2_chunk[:].rearrange("b (t q s) -> b t s q", t=TILES, s=S),
                                    AX.X, ALU.add).then_inc(p2_done, 1)
            dve.wait_ge(p2_turned, 1)
            nc.vector.tensor_copy(p2_t[:], y_bank[0][:]).then_inc(p2_t_done, 1)
            dve.wait_ge(y_full, 1)
            nc.vector.tensor_copy(y_row[:], y_bank[3][0:1, :]).then_inc(y_done, 1)


def kernel(**inputs):
    import numpy as np
    import concourse.bacc as bacc
    from concourse.bass_utils import run_bass_kernel_spmd

    nc = bacc.Bacc("TRN2", target_bir_lowering=False, num_devices=1)
    arrays = {}

    def dram(name, array):
        array = np.ascontiguousarray(array)
        arrays[name] = array
        return nc.dram_tensor(name, array.shape, mybir.dt.from_np(array.dtype), kind="ExternalInput").ap()

    jj, h = np.divmod(np.arange(ROWS), M)
    shift = STACK * np.arange(PAIR_TILES)[None, :] + jj[:, None]
    here = np.broadcast_to(h[:, None], shift.shape)
    there = (here + shift) % M
    w1 = np.transpose(np.asarray(inputs["L0_rec_W1"]), (1, 2, 0))
    w2 = np.transpose(np.asarray(inputs["L0_rec_W2"]), (1, 2, 0)).reshape(S, M * S)
    select = np.zeros((ROWS, PAIR_TILES + 1, ROWS), np.float32)
    for v in range(PAIR_TILES + 1):
        source = h if v == 0 else there[:, v - 1]
        for part in range(PARTS):
            select[part * M + source, v, np.arange(ROWS)] = 1.0
    def columns(name):
        return np.asarray(inputs[name]).reshape(-1, P).T

    table_names = [f"tbl_{f}" for f in range(M)]
    args = dict(
        ids=dram("ids", inputs["ids"]),
        tables=[dram(n, inputs[n]) for n in table_names],
        ctx_t=dram("ctx_t", np.transpose(np.asarray(inputs["dense_ctx"]))),
        w1_a=dram("w1_a", w1[here, there]), w1_b=dram("w1_b", w1[there, here]),
        b1=dram("b1", inputs["L0_rec_b1"]), w2_t=dram("w2_t", w2), b2=dram("b2", inputs["L0_rec_b2"]),
        select=dram("select", select.reshape(ROWS, -1)), ident=dram("ident", np.eye(P, dtype=np.float32)),
        w_top1=dram("w_top1", inputs["W_top1"]), b_top1=dram("b_top1", columns("b_top1")),
        w_top2=dram("w_top2", inputs["W_top2"]), b_top2=dram("b_top2", columns("b_top2")),
        w_top3=dram("w_top3", columns("W_top3")),
    )
    out = nc.dram_tensor("out", (inputs["ids"].shape[0], 1), F32, kind="ExternalOutput").ap()
    build(nc, out=out, **args)
    r = run_bass_kernel_spmd(nc, [arrays], core_ids=[0])
    return r.results[0]["out"]
```

```python
from contextlib import ExitStack

import concourse.bass as bass
from concourse import mybir

F32 = mybir.dt.float32
F32R = mybir.dt.float32r
BF16 = mybir.dt.bfloat16
I32 = mybir.dt.int32
ALU = mybir.AluOpType
ACT = mybir.ActivationFunctionType
AX = mybir.AxisListType

P = 128
M = 39
D = 16
S = 128
PARTS = 3
STACK = 3
ROWS = STACK * M
SHIFTS = (M + 1) // 2
PAIR_TILES = -(-SHIFTS // STACK)
LAST_ROWS = (SHIFTS - STACK * (PAIR_TILES - 1)) * M
CD = 4
CW = CD * P
FIELDS_IN_BANK = 4
BANKS = -(-M // FIELDS_IN_BANK)
SHORT = BANKS * FIELDS_IN_BANK - M
SLOTS = CD * BANKS
RING = 4
HALF = BANKS // 2
TILE_ACCS = HALF * FIELDS_IN_BANK - SHORT
ACCS = CD * TILE_ACCS

PLAIN_COPY_AT = 1
ROT_AT = [4 * t for t in range(PAIR_TILES)]
PRODUCT_AT = [4 * t + 4 for t in range(PAIR_TILES)]
PAIR_AT = [4 * t + 8 for t in range(PAIR_TILES)]
X1_COPY_AT = 35
X1_SPLIT_AT = 36
PART_AT = [17, 23, 29]
REST_AT = [20, 26]
TURN_AT = 34
TURN_COPY_AT = 37
STACK_AT = 38
FOLD_AT = 6


def fields_of(slot):
    width = FIELDS_IN_BANK - SHORT if slot == 0 else FIELDS_IN_BANK
    first = FIELDS_IN_BANK * slot - (SHORT if slot > 0 else 0)
    return first, width


def accs_before(slot):
    k, own = slot // BANKS, slot % BANKS // 2
    return k * TILE_ACCS + own * FIELDS_IN_BANK - (SHORT if own else 0)


def after(engine, semaphore, value):
    if isinstance(value, int) and value <= 0:
        return
    engine.wait_ge(semaphore, value)


def build(nc, ids, tables, ctx_t, w1_a, w1_b, b1, w2_t, b2, select, ident,
          w_top1, b_top1, w_top2, b_top2, w_top3, out):
    B = ids.shape[0]
    TILES = B // P
    CHUNKS_IN_TILE = D // CD
    CHUNKS = TILES * CHUNKS_IN_TILE
    PAIRS = CHUNKS // 2
    N1, N2 = w_top1.shape[1], w_top2.shape[1]
    T1, T2 = N1 // P, N2 // P
    CTX = ctx_t.shape[0]

    with ExitStack() as ctx:
        def sb(name, shape, dt=F32):
            return ctx.enter_context(nc.sbuf_tensor(name, shape, dt))

        def psum(name, shape, dt=F32):
            return ctx.enter_context(nc.psum_tensor(name, shape, dt))

        def sem(name):
            return ctx.enter_context(nc.semaphore(name))

        idx_all = sb("idx_all", [P, TILES, M], I32)
        select_f = sb("select_f", [ROWS, (PAIR_TILES + 1) * ROWS])
        select_b = sb("select_b", [ROWS, PAIR_TILES + 1, ROWS], BF16)
        ident_f = sb("ident_f", [P, P])
        ident_b = sb("ident_b", [P, P], BF16)
        w1_sym = sb("w1_sym", [ROWS, PAIR_TILES, S])
        w1_other = sb("w1_other", [ROWS, PAIR_TILES, S])
        w2_f = sb("w2_f", [S, M * S])
        w2_hi = sb("w2_hi", [S, M * S], F32R)
        w2_lo = sb("w2_lo", [S, M * S], F32R)
        b1_col = sb("b1_col", [S, 1])
        b2_rows = sb("b2_rows", [P, S])
        wt1 = sb("wt1", [P, 2, N1])
        wt1_ctx = sb("wt1_ctx", [CTX, N1])
        wt2 = sb("wt2", [P, T1, N2])
        wt3 = sb("wt3", [P, T2])
        bt1 = sb("bt1", [P, T1])
        bt2 = sb("bt2", [P, T2])
        ctx_sb = sb("ctx_sb", [CTX, B])
        gathered = sb("gathered", [P, M, TILES * D])
        parts = sb("parts", [P, CD, PARTS, M], BF16)
        staged = [sb(f"staged{i}", [P, CD, M]) for i in range(2)]
        rest = sb("rest", [P, PARTS - 1, CD, M])
        x0_chunk = [sb(f"x0_chunk{i}", [P, CD, M]) for i in range(2)]
        parts_t = sb("parts_t", [ROWS, CW], BF16)
        plain = sb("plain", [ROWS, CW])
        product = [sb(f"product{i}", [ROWS, CW]) for i in range(2)]
        x1 = sb("x1", [S, CW])
        x1_hi = [sb(f"x1_hi{i}", [S, CW], F32R) for i in range(2)]
        x1_lo = [sb(f"x1_lo{i}", [S, CW], F32R) for i in range(2)]
        prods = [sb(f"prods{i}", [P, HALF, FIELDS_IN_BANK * S]) for i in range(2)]
        pool_sum = sb("pool_sum", [P, 3, FIELDS_IN_BANK * S])
        sums = [sb(f"sums{i}", [P, 2 + FIELDS_IN_BANK, S]) for i in range(2)]
        x2 = sb("x2", [P, 2, S])
        p1_chunk = sb("p1_chunk", [S, CHUNKS * P])
        p2_chunk = sb("p2_chunk", [P, CHUNKS * S])
        p1_t = sb("p1_t", [S, B])
        p2 = sb("p2", [P, TILES, S])
        p2_t = sb("p2_t", [S, B])
        h1 = sb("h1", [P, T1, B])
        h2 = sb("h2", [P, T2, B])
        y_row = sb("y_row", [1, B])

        y_bank = [psum(f"y_bank{i}", [P, FIELDS_IN_BANK * S]) for i in range(RING)]
        rot_bank = [psum(f"rot_bank{i}", [P, CW]) for i in range(2)]
        turn_bank = psum("turn_bank", [P, CW])
        x1_bank = psum("x1_bank", [P, CW])
        mlp_bank = [turn_bank, x1_bank, *rot_bank]

        ids_in = sem("ids_in")
        w1_in = sem("w1_in")
        const_in = sem("const_in")
        w2_in = sem("w2_in")
        b2_in = sem("b2_in")
        top_in = sem("top_in")
        rows_in = [sem(f"rows_in{i}") for i in range(TILES)]
        out_sent = sem("out_sent")
        const_done = sem("const_done")
        w1_zeroed = sem("w1_zeroed")
        w1_done = sem("w1_done")
        w2_hi_done = sem("w2_hi_done")
        w2_lo_done = sem("w2_lo_done")
        x0_staged = sem("x0_staged")
        part_done = sem("part_done")
        rest_done = sem("rest_done")
        x0_done = sem("x0_done")
        turned = sem("turned")
        turn_copied = sem("turn_copied")
        rotated = sem("rotated")
        plain_done = sem("plain_done")
        product_done = sem("product_done")
        pairs_done = sem("pairs_done")
        x1_done = sem("x1_done")
        x1_used = sem("x1_used")
        y_even = sem("y_even")
        y_odd = sem("y_odd")
        acc_done = sem("acc_done")
        prods_done = sem("prods_done")
        pool_step = sem("pool_step")
        fold_step = sem("fold_step")
        p1_done = sem("p1_done")
        p2_done = sem("p2_done")
        p2_turned = sem("p2_turned")
        p2_t_done = sem("p2_t_done")
        h1_full = sem("h1_full")
        h1_done = sem("h1_done")
        h2_full = sem("h2_full")
        h2_done = sem("h2_done")
        y_full = sem("y_full")
        y_done = sem("y_done")

        POOL_STEPS = 4
        LAST_POOL = POOL_STEPS
        def chunk_pairs(engine, chunk):
            for half in range(2):
                chunk(half, half)
            with engine.Fori(1, PAIRS - 1) as pair:
                for half in range(2):
                    chunk(pair * 2 + half, half)
            for half in range(2):
                chunk(CHUNKS - 2 + half, half)

        def exists(c):
            return not (isinstance(c, int) and c >= CHUNKS)

        block = ctx.enter_context(nc.Block())

        @block.sync
        def _(sp):
            sp.dma_start(idx_all[:], ids.rearrange("(t p) f -> p t f", p=P)).then_inc(ids_in, 16)
            sp.dma_start(select_f[:], select).then_inc(const_in, 16)
            sp.dma_start(ident_f[:], ident).then_inc(const_in, 16)
            sp.dma_start(w1_sym[:], w1_a).then_inc(w1_in, 16)
            sp.dma_start(w1_other[:], w1_b).then_inc(w1_in, 16)
            sp.dma_start(b1_col[:], b1.rearrange("(s a) -> s a", a=1)).then_inc(w1_in, 16)
            sp.dma_start(w2_f[:], w2_t).then_inc(w2_in, 16)
            sp.dma_start(b2_rows[:], b2.rearrange("(a s) -> a s", a=1).broadcast_to([P, S])).then_inc(b2_in, 16)
            sp.dma_start(wt1[:], w_top1[0:2 * P, :].rearrange("(t p) n -> p t n", p=P)).then_inc(top_in, 16)
            sp.dma_start(wt1_ctx[:], w_top1[2 * P:2 * P + CTX, :]).then_inc(top_in, 16)
            sp.dma_start(wt2[:], w_top2.rearrange("(t p) n -> p t n", p=P)).then_inc(top_in, 16)
            sp.dma_start(wt3[:], w_top3).then_inc(top_in, 16)
            sp.dma_start(bt1[:], b_top1).then_inc(top_in, 16)
            sp.dma_start(bt2[:], b_top2).then_inc(top_in, 16)
            sp.dma_start(ctx_sb[:], ctx_t).then_inc(top_in, 16)
            sp.wait_ge(y_done, 1)
            sp.dma_start(out.rearrange("b a -> a b"), y_row[:]).then_inc(out_sent, 16)
            sp.wait_ge(out_sent, 16)
        TOP_DMAS = 7

        @block.gpsimd
        def _(pool):
            def gather(tile, field):
                nc.gpsimd.indirect_dma_start(
                    out=gathered[:, field, tile * D:(tile + 1) * D], out_offset=None, in_=tables[field],
                    in_offset=bass.IndirectOffsetOnAxis(ap=idx_all[:, tile, field:field + 1], axis=0),
                ).then_inc(rows_in[tile], 16)

            def stage(c):
                pool.wait_ge(rows_in[c // CHUNKS_IN_TILE], 16 * M)
                after(pool, part_done, (c - 1) * PARTS)
                after(pool, x0_done, c - 1)
                nc.gpsimd.tensor_copy(staged[c % 2][:], gathered[:, :, c * CD:(c + 1) * CD].rearrange("p f d -> p d f")
                                      ).then_inc(x0_staged, 1)

            def sum_products(n, k):
                bank = prods[k % 2]
                total = sums[k % 2][:, 2:, :].rearrange("p a s -> p (a s)")
                step = n * POOL_STEPS
                pool.wait_ge(prods_done, n * HALF + 2)
                nc.gpsimd.tensor_tensor(pool_sum[:, 0], bank[:, 0], bank[:, 1], ALU.add).then_inc(pool_step, 1)
                pool.wait_ge(prods_done, n * HALF + 4)
                nc.gpsimd.tensor_tensor(pool_sum[:, 1], bank[:, 2], bank[:, 3], ALU.add).then_inc(pool_step, 1)
                pool.wait_ge(pool_step, step + 2)
                nc.gpsimd.tensor_tensor(pool_sum[:, 2], pool_sum[:, 0], pool_sum[:, 1], ALU.add).then_inc(pool_step, 1)
                pool.wait_ge(prods_done, n * HALF + 5)
                pool.wait_ge(pool_step, step + 3)
                after(pool, fold_step, n * 2 - 3)
                nc.gpsimd.tensor_tensor(total, pool_sum[:, 2], bank[:, 4], ALU.add).then_inc(pool_step, 1)

            def issued_by(n):
                if n < 0:
                    return M
                tile, at = divmod(n + D - LEAD, D)
                if tile == 0:
                    return M + EARLY + -(-(M - EARLY) * (at - D + LEAD + 1) // LEAD)
                return min(TILES * M, M * (tile + 1) + -(-M * (at + 1) // D))

            LEAD = 9
            EARLY = 11
            pool.wait_ge(ids_in, 16)
            for field in range(M):
                gather(0, field)
            stage(0)
            stage(1)
            issued = M
            for g in range(issued, issued + EARLY):
                gather(*divmod(g, M))
            issued += EARLY
            for n in range(TILES * D):
                upto = issued_by(n)
                for g in range(issued, upto):
                    gather(*divmod(g, M))
                issued = upto
                sum_products(n, n % CD)
                if n % CD == 0 and n // CD + 2 < CHUNKS:
                    stage(n // CD + 2)

        @block.tensor
        def _(pe):
            def turn(c):
                pe.wait_ge(part_done, c * PARTS + PARTS)
                after(pe, turn_copied, c)
                for k in range(CD):
                    last = nc.tensor.matmul(
                        turn_bank[0:ROWS, k * P:(k + 1) * P], parts[:, k].rearrange("p i f -> p (i f)"),
                        ident_b[:], start=True, stop=True)
                last.then_inc(turned, 1)

            def rotate(c, v):
                if v == 0:
                    pe.wait_ge(turn_copied, c + 1)
                if v == 2:
                    pe.wait_ge(plain_done, c + 1)
                else:
                    after(pe, product_done, c * PAIR_TILES + (v - 1 if v < 2 else v - 2))
                nc.tensor.matmul(rot_bank[v % 2][0:ROWS, :], select_b[:, v, :], parts_t[:],
                                 start=True, stop=True).then_inc(rotated, 1)

            def contract_pairs(c, t):
                if t == 0:
                    after(pe, x1_done, c * 2)
                pe.wait_ge(product_done, c * PAIR_TILES + (t + 1))
                rows = LAST_ROWS if t == PAIR_TILES - 1 else ROWS
                z = product[t % 2]
                nc.tensor.matmul(x1_bank[:], w1_sym[0:rows, t, :], z[0:rows, :],
                                 start=(t == 0), stop=(t == PAIR_TILES - 1)).then_inc(pairs_done, 1)

            def chunk(c, half):
                pe.wait_ge(x1_done, c * 2 + 2)
                pe.wait_ge(x1_used, c * 2 + 1)
                for slot in range(SLOTS):
                    if exists(c + 2):
                        if slot == TURN_AT:
                            turn(c + 2)
                        if slot == STACK_AT:
                            rotate(c + 2, 0)
                    if exists(c + 1):
                        if slot in ROT_AT:
                            rotate(c + 1, ROT_AT.index(slot) + 1)
                        if slot in PAIR_AT:
                            contract_pairs(c + 1, PAIR_AT.index(slot))
                    k, j = slot // BANKS, slot // 2
                    first, width = fields_of(slot % BANKS)
                    cols = slice(first * S, (first + width) * S)
                    hi = x1_hi[half][:, k * P:(k + 1) * P]
                    lo = x1_lo[half][:, k * P:(k + 1) * P]
                    y = y_bank[slot % RING][:, 0:width * S]
                    if slot % 2 == 0:
                        after(pe, acc_done, c * ACCS + accs_before(slot - 2))
                    else:
                        after(pe, prods_done, c * (SLOTS // 2) + (j - 1))
                    nc.tensor.matmul(y, hi, w2_hi[:, cols], start=True, stop=False)
                    nc.tensor.matmul(y, hi, w2_lo[:, cols], start=False, stop=False)
                    nc.tensor.matmul(y, lo, w2_hi[:, cols], start=False, stop=True
                                     ).then_inc(y_even if slot % 2 == 0 else y_odd, 1)

            pe.wait_ge(const_done, 2)
            turn(0)
            rotate(0, 0)
            rotate(0, 1)
            pe.wait_ge(w1_done, 1)
            for t in range(PAIR_TILES):
                if t + 1 < PAIR_TILES:
                    rotate(0, t + 2)
                contract_pairs(0, t)
            turn(1)
            rotate(1, 0)
            pe.wait_ge(w2_hi_done, 1)
            pe.wait_ge(w2_lo_done, 1)
            chunk_pairs(pe, chunk)

            pe.wait_ge(top_in, 16 * TOP_DMAS)
            pe.wait_ge(p1_done, 1)
            for t in range(T1):
                cols = slice(t * P, (t + 1) * P)
                nc.tensor.matmul(mlp_bank[t][:], wt1[:, 0, cols], p1_t[:], start=True, stop=False)
                nc.tensor.matmul(mlp_bank[t][:], wt1_ctx[:, cols], ctx_sb[:], start=False, stop=False)
            pe.wait_ge(p2_done, 1)
            for b in range(TILES):
                last = nc.tensor.transpose(y_bank[0][:, b * P:(b + 1) * P], p2[:, b, :], ident_f[:])
            last.then_inc(p2_turned, 1)
            pe.wait_ge(p2_t_done, 1)
            for t in range(T1):
                nc.tensor.matmul(mlp_bank[t][:], wt1[:, 1, t * P:(t + 1) * P], p2_t[:],
                                 start=False, stop=True).then_inc(h1_full, 1)
            for t in range(T1):
                pe.wait_ge(h1_done, t + 1)
                for u in range(T2):
                    last = nc.tensor.matmul(y_bank[1 + u][:], wt2[:, t, u * P:(u + 1) * P], h1[:, t, :],
                                            start=(t == 0), stop=(t == T1 - 1))
                    if t == T1 - 1:
                        last.then_inc(h2_full, 1)
            for u in range(T2):
                pe.wait_ge(h2_done, u + 1)
                last = nc.tensor.matmul(y_bank[3][0:1, :], wt3[:, u:u + 1], h2[:, u, :],
                                        start=(u == 0), stop=(u == T2 - 1))
            last.then_inc(y_full, 1)

        @block.scalar
        def _(act):
            def scalars(c, half):
                act.wait_ge(x0_staged, c + 1)
                after(act, acc_done, (c - 1) * ACCS)
                after(act, prods_done, (c - 1) * (SLOTS // 2))
                nc.scalar.activation(x0_chunk[half][:], staged[half][:], ACT.Copy).then_inc(x0_done, 1)

            def part(c, half, i):
                if i == 0:
                    act.wait_ge(x0_staged, c + 1)
                    after(act, turned, c)
                else:
                    act.wait_ge(rest_done, c * (PARTS - 1) + i)
                nc.scalar.activation(parts[:, :, i, :], staged[half][:] if i == 0 else rest[:, i - 1],
                                     ACT.Copy).then_inc(part_done, 1)

            def copy_turned(c):
                act.wait_ge(turned, c + 1)
                after(act, rotated, c * (PAIR_TILES + 1))
                nc.scalar.activation(parts_t[:], turn_bank[0:ROWS, :], ACT.Copy).then_inc(turn_copied, 1)

            def copy_plain(c):
                act.wait_ge(rotated, c * (PAIR_TILES + 1) + 1)
                after(act, product_done, c * PAIR_TILES)
                nc.scalar.activation(plain[:], rot_bank[0][0:ROWS, :], ACT.Copy).then_inc(plain_done, 1)

            def finish_x1(c, half):
                act.wait_ge(pairs_done, (c + 1) * PAIR_TILES)
                after(act, x1_used, c * 2)
                nc.scalar.activation(x1[:], x1_bank[:], ACT.Relu, bias=b1_col[:]).then_inc(x1_done, 1)
                nc.scalar.activation(x1_hi[half][:], x1_bank[:], ACT.Relu, bias=b1_col[:]).then_inc(x1_done, 1)

            def chunk(c, half):
                act.wait_ge(x0_done, c + 1)
                for slot in range(1, SLOTS, 2):
                    if exists(c + 2):
                        if slot in PART_AT:
                            part(c + 2, half, PART_AT.index(slot))
                        if slot == TURN_COPY_AT:
                            copy_turned(c + 2)
                    if exists(c + 1):
                        if slot == PLAIN_COPY_AT:
                            copy_plain(c + 1)
                            scalars(c + 1, 1 - half)
                        if slot == X1_COPY_AT:
                            finish_x1(c + 1, 1 - half)
                    k, j = slot // BANKS, slot // 2
                    first, width = fields_of(slot % BANKS)
                    act.wait_ge(y_odd, c * (SLOTS // 2) + (j + 1))
                    if slot % BANKS == 1:
                        after(act, pool_step, (c * CD + (k - 1)) * POOL_STEPS)
                    for f in range(width):
                        last = nc.scalar.activation(
                            prods[k % 2][:, j % HALF, f * S:(f + 1) * S],
                            y_bank[slot % RING][:, f * S:(f + 1) * S], ACT.Copy,
                            scale=x0_chunk[half][:, k, first + f:first + f + 1])
                    last.then_inc(prods_done, 1)

            act.wait_ge(const_in, 32)
            nc.scalar.activation(select_b[:].rearrange("p v r -> p (v r)"), select_f[:],
                                 ACT.Copy).then_inc(const_done, 1)
            nc.scalar.activation(ident_b[:], ident_f[:], ACT.Copy).then_inc(const_done, 1)
            act.wait_ge(w2_in, 16)
            nc.scalar.activation(w2_hi[:], w2_f[:], ACT.Copy).then_inc(w2_hi_done, 1)
            act.wait_ge(w1_in, 48)
            for i in range(PARTS):
                part(0, 0, i)
            copy_turned(0)
            copy_plain(0)
            for i in range(PARTS):
                part(1, 1, i)
            scalars(0, 0)
            copy_turned(1)
            finish_x1(0, 0)
            chunk_pairs(act, chunk)

            act.wait_ge(top_in, 16 * TOP_DMAS)
            for t in range(T1):
                act.wait_ge(h1_full, t + 1)
                nc.scalar.activation(h1[:, t, :], mlp_bank[t][:], ACT.Relu, bias=bt1[:, t:t + 1]).then_inc(h1_done, 1)
            for u in range(T2):
                act.wait_ge(h2_full, u + 1)
                nc.scalar.activation(h2[:, u, :], y_bank[1 + u][:], ACT.Relu, bias=bt2[:, u:u + 1]).then_inc(h2_done, 1)

        @block.vector
        def _(dve):
            def leave(c, half, i):
                dve.wait_ge(part_done, c * PARTS + (i + 1))
                after(dve, part_done, c * PARTS)
                nc.vector.tensor_tensor(rest[:, i], staged[half][:] if i == 0 else rest[:, i - 1], parts[:, :, i, :],
                                        ALU.subtract).then_inc(rest_done, 1)

            def multiply_pairs(c, t):
                dve.wait_ge(rotated, c * (PAIR_TILES + 1) + (t + 2))
                dve.wait_ge(plain_done, c + 1)
                after(dve, pairs_done, c * PAIR_TILES + (t - 1 if t >= 2 else 0))
                nc.vector.tensor_tensor(product[t % 2][:], rot_bank[(t + 1) % 2][0:ROWS, :], plain[:],
                                        ALU.mult).then_inc(product_done, 1)

            def split_x1(c, half):
                dve.wait_ge(x1_done, c * 2 + 2)
                nc.vector.tensor_tensor(x1_lo[half][:], x1[:], x1_hi[half][:].bitcast(F32),
                                        ALU.subtract).then_inc(x1_used, 1)
                nc.vector.tensor_reduce(p1_chunk[:, bass.ds(c * P, P)], x1[:].rearrange("h (d b) -> h b d", d=CD),
                                        AX.X, ALU.add).then_inc(x1_used, 1)

            def fold(c, k):
                n = c * CD + k
                here = p2_chunk[:, bass.ds(c * S, S)]
                dve.wait_ge(pool_step, n * POOL_STEPS + LAST_POOL)
                dve.wait_ge(acc_done, c * ACCS + (k + 1) * TILE_ACCS)
                nc.vector.tensor_reduce(x2[:, k % 2, :], sums[k % 2][:].rearrange("p a s -> p s a"),
                                        AX.X, ALU.add).then_inc(fold_step, 1)
                dve.wait_ge(fold_step, n * 2 + 1)
                if k == 0:
                    nc.vector.tensor_scalar(here, x2[:, k % 2, :], 0.0, None, ALU.max).then_inc(fold_step, 1)
                else:
                    nc.vector.scalar_tensor_tensor(out=here, in0=x2[:, k % 2, :], scalar=0.0, in1=here,
                                                   op0=ALU.max, op1=ALU.add).then_inc(fold_step, 1)

            def chunk(c, half):
                dve.wait_ge(x0_done, c + 1)
                for slot in range(0, SLOTS, 2):
                    if exists(c + 2) and slot in REST_AT:
                        leave(c + 2, half, REST_AT.index(slot))
                    if exists(c + 1):
                        if slot in PRODUCT_AT:
                            multiply_pairs(c + 1, PRODUCT_AT.index(slot))
                        if slot == X1_SPLIT_AT:
                            split_x1(c + 1, 1 - half)
                    k, j = slot // BANKS, slot // 2
                    if slot % BANKS == FOLD_AT:
                        if k > 0:
                            fold(c, k - 1)
                        elif not (isinstance(c, int) and c == 0):
                            fold(c - 1, CD - 1)
                    first, width = fields_of(slot % BANKS)
                    dve.wait_ge(y_even, c * (SLOTS // 2) + (j + 1))
                    for f in range(width):
                        y = y_bank[slot % RING][:, f * S:(f + 1) * S]
                        x = x0_chunk[half][:, k, first + f:first + f + 1]
                        acc = sums[k % 2][:, (accs_before(slot) + f - k * TILE_ACCS) % 2, :]
                        after(dve, acc_done, c * ACCS + (accs_before(slot) + f - 1))
                        if slot % BANKS == 0 and f == 0:
                            after(dve, fold_step, (c * CD + k) * 2 - 3)
                        if slot % BANKS == 0 and f == 1:
                            nc.vector.tensor_scalar(acc, y, x, None, ALU.mult).then_inc(acc_done, 1)
                        else:
                            start = slot % BANKS == 0 and f == 0
                            nc.vector.scalar_tensor_tensor(out=acc, in0=y, scalar=x, in1=b2_rows[:] if start else acc,
                                                           op0=ALU.mult, op1=ALU.add).then_inc(acc_done, 1)

            dve.wait_ge(w1_in, 48)
            nc.vector.memset(w1_other[0:M, 0, :], 0.0).then_inc(w1_zeroed, 1)
            dve.wait_ge(w1_zeroed, 1)
            nc.vector.tensor_tensor(w1_sym[:], w1_sym[:], w1_other[:], ALU.add).then_inc(w1_done, 1)
            dve.wait_ge(w2_hi_done, 1)
            nc.vector.tensor_tensor(w2_lo[:], w2_f[:], w2_hi[:].bitcast(F32), ALU.subtract).then_inc(w2_lo_done, 1)
            for i in range(PARTS - 1):
                leave(0, 0, i)
            for t in range(PAIR_TILES):
                multiply_pairs(0, t)
                if t < PARTS - 1:
                    leave(1, 1, t)
            split_x1(0, 0)
            dve.wait_ge(b2_in, 16)
            chunk_pairs(dve, chunk)

            dve.wait_ge(x1_used, CHUNKS * 2)
            nc.vector.tensor_reduce(p1_t[:].rearrange("h (t b) -> h t b", t=TILES),
                                    p1_chunk[:].rearrange("h (t q b) -> h t b q", t=TILES, b=P),
                                    AX.X, ALU.add).then_inc(p1_done, 1)
            fold(CHUNKS - 1, CD - 1)
            dve.wait_ge(fold_step, CHUNKS * CD * 2)
            nc.vector.tensor_reduce(p2[:], p2_chunk[:].rearrange("b (t q s) -> b t s q", t=TILES, s=S),
                                    AX.X, ALU.add).then_inc(p2_done, 1)
            dve.wait_ge(p2_turned, 1)
            nc.vector.tensor_copy(p2_t[:], y_bank[0][:]).then_inc(p2_t_done, 1)
            dve.wait_ge(y_full, 1)
            nc.vector.tensor_copy(y_row[:], y_bank[3][0:1, :]).then_inc(y_done, 1)


def kernel(**inputs):
    import numpy as np
    import concourse.bacc as bacc
    from concourse.bass_utils import run_bass_kernel_spmd

    nc = bacc.Bacc("TRN2", target_bir_lowering=False, num_devices=1)
    arrays = {}

    def dram(name, array):
        array = np.ascontiguousarray(array)
        arrays[name] = array
        return nc.dram_tensor(name, array.shape, mybir.dt.from_np(array.dtype), kind="ExternalInput").ap()

    jj, h = np.divmod(np.arange(ROWS), M)
    shift = STACK * np.arange(PAIR_TILES)[None, :] + jj[:, None]
    here = np.broadcast_to(h[:, None], shift.shape)
    there = (here + shift) % M
    w1 = np.transpose(np.asarray(inputs["L0_rec_W1"]), (1, 2, 0))
    w2 = np.transpose(np.asarray(inputs["L0_rec_W2"]), (1, 2, 0)).reshape(S, M * S)
    select = np.zeros((ROWS, PAIR_TILES + 1, ROWS), np.float32)
    for v in range(PAIR_TILES + 1):
        source = h if v == 0 else there[:, v - 1]
        for part in range(PARTS):
            select[part * M + source, v, np.arange(ROWS)] = 1.0
    def columns(name):
        return np.asarray(inputs[name]).reshape(-1, P).T

    table_names = [f"tbl_{f}" for f in range(M)]
    args = dict(
        ids=dram("ids", inputs["ids"]),
        tables=[dram(n, inputs[n]) for n in table_names],
        ctx_t=dram("ctx_t", np.transpose(np.asarray(inputs["dense_ctx"]))),
        w1_a=dram("w1_a", w1[here, there]), w1_b=dram("w1_b", w1[there, here]),
        b1=dram("b1", inputs["L0_rec_b1"]), w2_t=dram("w2_t", w2), b2=dram("b2", inputs["L0_rec_b2"]),
        select=dram("select", select.reshape(ROWS, -1)), ident=dram("ident", np.eye(P, dtype=np.float32)),
        w_top1=dram("w_top1", inputs["W_top1"]), b_top1=dram("b_top1", columns("b_top1")),
        w_top2=dram("w_top2", inputs["W_top2"]), b_top2=dram("b_top2", columns("b_top2")),
        w_top3=dram("w_top3", columns("W_top3")),
    )
    out = nc.dram_tensor("out", (inputs["ids"].shape[0], 1), F32, kind="ExternalOutput").ap()
    build(nc, out=out, **args)
    r = run_bass_kernel_spmd(nc, [arrays], core_ids=[0])
    return r.results[0]["out"]
```

```python
from contextlib import ExitStack

import concourse.bass as bass
from concourse import mybir

F32 = mybir.dt.float32
F32R = mybir.dt.float32r
I32 = mybir.dt.int32
ALU = mybir.AluOpType
ACT = mybir.ActivationFunctionType
AX = mybir.AxisListType

P = 128
M = 39
D = 16
S = 128
STACK = 3
ROWS = STACK * M
SHIFTS = (M + 1) // 2
PAIR_TILES = -(-SHIFTS // STACK)
WINDOW = M + STACK * PAIR_TILES - 1
SPLIT = slice(1, 6, 2)
SPLIT_TILES = [*range(PAIR_TILES)[SPLIT]]
LAST_ROWS = (SHIFTS - STACK * (PAIR_TILES - 1)) * M
CD = 4
CW = CD * P
FIELDS_IN_BANK = 4
BANKS = -(-M // FIELDS_IN_BANK)
SHORT = BANKS * FIELDS_IN_BANK - M
SLOTS = CD * BANKS
OWNER = "VSSVSSVSVS"
RING = {"V": 4, "S": 3}
V_BANKS, S_BANKS = OWNER.count("V"), OWNER.count("S")
TILE_ACCS = V_BANKS * FIELDS_IN_BANK - SHORT
ACCS = CD * TILE_ACCS
SUMS = 2 + FIELDS_IN_BANK + FIELDS_IN_BANK
POOL_SUMS = 2
LAST_BANK = POOL_SUMS + FIELDS_IN_BANK

PRODUCT_AT = [2, 0, 10, 5, 17, 12, 23]
PAIR_HI_AT, PAIR_LO_AT = [5, 11, 18], [8, 15, 21]
PAIR_AT = [10, 15, 18, 23, 25, 28, 32]
PRODUCT_ORDER = sorted(range(PAIR_TILES), key=lambda t: PRODUCT_AT[t])
SCALARS_AT = 24
X1_COPY_AT = 33
X1_SPLIT_AT, X1_SUM_AT = 34, 36
TURN_AT, TURN_COPY_AT = 1, 3
REST_PRODUCT_AT, REST_PAIR_AT, REST_COPY_AT = 3, 6, 7
REST_SPLIT_AT, REST_SUM_AT = 8, 12
PRODUCT_AT_0 = [11, 9, 16, 13, 21, 18, 24]
PAIR_HI_AT_0, PAIR_LO_AT_0 = [11, 15, 20], [15, 20, 23]
PAIR_AT_0 = [17, 19, 22, 24, 27, 29, 32]
TURN_AT_0, TURN_COPY_AT_0 = 10, 11
FOLD_AT = 6

MLP_AT = [5 + 4 * step for step in range(8)]
MLP_READ_AT = [at + 1 for at in MLP_AT]
P1_AT = 1


def fields_of(slot):
    width = FIELDS_IN_BANK - SHORT if slot == 0 else FIELDS_IN_BANK
    first = FIELDS_IN_BANK * slot - (SHORT if slot > 0 else 0)
    return first, width


def nth(slot):
    k, own = divmod(slot, BANKS)
    return k * OWNER.count(OWNER[own]) + OWNER[:own].count(OWNER[own])


def accs_before(slot):
    k, own = divmod(slot, V_BANKS)
    return k * TILE_ACCS + own * FIELDS_IN_BANK - (SHORT if own else 0)


def products_by(c, t):
    return t + 1 if isinstance(c, int) and c == 0 else c * PAIR_TILES + (PRODUCT_ORDER.index(t) + 1)


def after(engine, semaphore, value):
    if isinstance(value, int) and value <= 0:
        return
    engine.wait_ge(semaphore, value)


def build(nc, ids, tables, ctx_t, rotation, w1_a, w1_b, b1, w2_t, b2, ident,
          w_top1, b_top1, w_top2, b_top2, w_top3, x0_rows, out):
    B = ids.shape[0]
    TILES = B // P
    CHUNKS_IN_TILE = D // CD
    CHUNKS = TILES * CHUNKS_IN_TILE
    PAIRS = CHUNKS // 2
    N1, N2 = w_top1.shape[1], w_top2.shape[1]
    T1, T2 = N1 // P, N2 // P
    CTX = ctx_t.shape[0]
    EARLY_TILES = TILES - 1
    early, late = slice(0, EARLY_TILES * P), slice(EARLY_TILES * P, B)
    TURN_STEP, H1_STEP, H2_STEP, ROW_STEP = 0, 1, 1 + T1, 1 + T1 + T2

    with ExitStack() as ctx:
        def sb(name, shape, dt=F32):
            return ctx.enter_context(nc.sbuf_tensor(name, shape, dt))

        def psum(name, shape, dt=F32):
            return ctx.enter_context(nc.psum_tensor(name, shape, dt))

        def sem(name):
            return ctx.enter_context(nc.semaphore(name))

        idx_all = sb("idx_all", [P, TILES, M], I32)
        ident_f = sb("ident_f", [P, P])
        w1_sym = sb("w1_sym", [ROWS, PAIR_TILES, S])
        w1_other = sb("w1_other", [ROWS, PAIR_TILES, S])
        w1_hi = sb("w1_hi", [ROWS, len(SPLIT_TILES), S], F32R)
        w1_lo = sb("w1_lo", [ROWS, len(SPLIT_TILES), S], F32R)
        w2_f = sb("w2_f", [S, M * S])
        w2_hi = sb("w2_hi", [S, M * S], F32R)
        w2_lo = sb("w2_lo", [S, M * S], F32R)
        b1_col = sb("b1_col", [S, 1])
        b2_rows = sb("b2_rows", [P, S])
        wt1 = sb("wt1", [P, 2, N1])
        wt1_ctx = sb("wt1_ctx", [CTX, N1])
        wt2 = sb("wt2", [P, T1, N2])
        wt3 = sb("wt3", [P, T2])
        bt1 = sb("bt1", [P, T1])
        bt2 = sb("bt2", [P, T2])
        ctx_sb = sb("ctx_sb", [CTX, B])
        gathered = sb("gathered", [P, M, TILES * D])
        staged = [sb(f"staged{i}", [P, CD, M]) for i in range(2)]
        x0_chunk = [sb(f"x0_chunk{i}", [P, CD, M]) for i in range(2)]
        x0_t = [sb(f"x0_t{i}", [2 * M, CW // 2]) for i in range(2)]
        plain = [sb(f"plain{i}", [ROWS, CW]) for i in range(2)]
        rotated = [sb(f"rotated{i}", [ROWS, PAIR_TILES, CW]) for i in range(2)]
        pair_hi = [sb(f"pair_hi{i}", [ROWS, CW], F32R) for i in range(len(SPLIT_TILES))]
        pair_lo = [sb(f"pair_lo{i}", [ROWS, CW], F32R) for i in range(len(SPLIT_TILES))]
        x1 = sb("x1", [S, CW])
        x1_hi = [sb(f"x1_hi{i}", [S, CW], F32R) for i in range(2)]
        x1_lo = [sb(f"x1_lo{i}", [S, CW], F32R) for i in range(2)]
        prods = [sb(f"prods{i}", [P, S_BANKS - 1, FIELDS_IN_BANK * S]) for i in range(2)]
        pool_sum = sb("pool_sum", [P, 3, FIELDS_IN_BANK * S])
        sums = [sb(f"sums{i}", [P, SUMS, S]) for i in range(2)]
        x2 = sb("x2", [P, 2, S])
        p1_chunk = sb("p1_chunk", [S, CHUNKS * P])
        p2_chunk = sb("p2_chunk", [P, CHUNKS * S])
        p2 = sb("p2", [P, EARLY_TILES, S])
        h1 = w2_f[:, 0:T1 * B].rearrange("p (t b) -> p t b", t=T1)
        h2 = w2_f[:, T1 * B:(T1 + T2) * B].rearrange("p (t b) -> p t b", t=T2)
        p1_t, p2_t, y_row = (w2_f[:, (T1 + T2 + i) * B:(T1 + T2 + i + 1) * B] for i in range(3))

        y_bank = {o: [psum(f"y_bank_{o}{i}", [P, FIELDS_IN_BANK * S]) for i in range(RING[o])] for o in "VS"}
        first_rotation = prods[1][0:M].rearrange("p a s -> p (a s)")[:, 0:(PAIR_TILES + 1) * ROWS].rearrange(
            "p (t r) -> p t r", r=ROWS)
        first_pairs = prods[0][0:ROWS].rearrange("p a s -> p (a s)")[:, 0:PAIR_TILES * P].rearrange(
            "p (t b) -> p t b", b=P)
        first_plain = prods[0][0:ROWS].rearrange("p a s -> p (a s)")[:, PAIR_TILES * P:(PAIR_TILES + 1) * P]
        x1_bank = psum("x1_bank", [P, CW])
        turn_bank = [x1_bank[0:2 * M, i * (CW // 2):(i + 1) * (CW // 2)] for i in range(2)]
        rotation_bank = y_bank["V"][0:2]
        h1_bank = y_bank["V"]
        p2_bank, *h2_bank = y_bank["S"]

        ids_in = sem("ids_in")
        w1_in = sem("w1_in")
        ident_in = sem("ident_in")
        w2_in = sem("w2_in")
        b2_in = sem("b2_in")
        top_in = sem("top_in")
        rows_in = [sem(f"rows_in{i}") for i in range(TILES)]
        out_sent = sem("out_sent")
        w1_zeroed = sem("w1_zeroed")
        w1_done = sem("w1_done")
        w1_hi_done = sem("w1_hi_done")
        w1_lo_done = sem("w1_lo_done")
        w2_hi_done = sem("w2_hi_done")
        w2_lo_done = sem("w2_lo_done")
        x0_staged = sem("x0_staged")
        x0_done = sem("x0_done")
        turned = sem("turned")
        turn_copied = sem("turn_copied")
        x0_sent = sem("x0_sent")
        rotation_in = sem("rotation_in")
        rotated_full = sem("rotated_full")
        first_plain_done = sem("first_plain_done")
        first_product_done = sem("first_product_done")
        first_pairs_done = sem("first_pairs_done")
        first_x1_done = sem("first_x1_done")
        first_lo_done = sem("first_lo_done")
        first_in = [sem(f"first_in{i}") for i in range(2)]
        rotated_in = [sem(f"rotated_in{i}") for i in range(2)]
        product_done = sem("product_done")
        pair_hi_done = sem("pair_hi_done")
        pair_lo_done = sem("pair_lo_done")
        pairs_done = sem("pairs_done")
        x1_done = sem("x1_done")
        x1_used = sem("x1_used")
        y_full = {o: sem(f"y_full_{o}") for o in "VS"}
        acc_done = sem("acc_done")
        prods_done = sem("prods_done")
        pool_step = sem("pool_step")
        fold_step = sem("fold_step")
        early_summed = sem("early_summed")
        p1_done = sem("p1_done")
        p2_done = sem("p2_done")
        p2_turned = sem("p2_turned")
        p2_t_done = sem("p2_t_done")
        h1_full = sem("h1_full")
        h1_done = sem("h1_done")
        h2_full = sem("h2_full")
        h2_done = sem("h2_done")
        row_full = sem("row_full")
        y_done = sem("y_done")

        POOL_STEPS = 3
        EARLY_SUMS = 2 * (CHUNKS_IN_TILE - 1)
        EARLY_SUMS_AT = (EARLY_TILES * CHUNKS_IN_TILE + 1) * CD
        LAST_TILE = CHUNKS * CD - 1
        TOP_DMAS = 7
        SENT = 4 * 16
        LATER_MATRICES = [*range(PAIR_TILES + 1)][FIELDS_IN_BANK:]
        EARLIER_MATRICES = [*range(PAIR_TILES + 1)][:FIELDS_IN_BANK]
        REST = slice(P, CW)
        FIRST_TILES = 3

        def is_last(n):
            return isinstance(n, int) and n == LAST_TILE

        def is_first(c):
            return isinstance(c, int) and c == 0

        def chunk_pairs(engine, chunk):
            for half in range(2):
                chunk(half, half)
            with engine.Fori(1, PAIRS - 1) as pair:
                for half in range(2):
                    chunk(pair * 2 + half, half)
            for half in range(2):
                chunk(CHUNKS - 2 + half, half)

        def exists(c):
            return not (isinstance(c, int) and c >= CHUNKS)

        block = ctx.enter_context(nc.Block())

        @block.sync
        def _(sp):
            sp.dma_start(idx_all[:], ids.rearrange("(t p) f -> p t f", p=P)).then_inc(ids_in, 16)
            sp.dma_start(ident_f[:], ident).then_inc(ident_in, 16)
            sp.dma_start(w1_sym[:], w1_a).then_inc(w1_in, 16)
            sp.dma_start(w1_other[:], w1_b).then_inc(w1_in, 16)
            sp.dma_start(first_rotation, rotation).then_inc(rotation_in, 16)
            sp.dma_start(b1_col[:], b1.rearrange("(s a) -> s a", a=1)).then_inc(w1_in, 16)
            sp.dma_start(w2_f[:], w2_t).then_inc(w2_in, 16)
            sp.dma_start(b2_rows[:], b2.rearrange("(a s) -> a s", a=1).broadcast_to([P, S])).then_inc(b2_in, 16)
            sp.dma_start(wt1[:], w_top1[0:2 * P, :].rearrange("(t p) n -> p t n", p=P)).then_inc(top_in, 16)
            sp.dma_start(wt1_ctx[:], w_top1[2 * P:2 * P + CTX, :]).then_inc(top_in, 16)
            sp.dma_start(wt2[:], w_top2.rearrange("(t p) n -> p t n", p=P)).then_inc(top_in, 16)
            sp.dma_start(wt3[:], w_top3).then_inc(top_in, 16)
            sp.dma_start(bt1[:], b_top1).then_inc(top_in, 16)
            sp.dma_start(bt2[:], b_top2).then_inc(top_in, 16)
            sp.dma_start(ctx_sb[:], ctx_t).then_inc(top_in, 16)

            def windows(half, first, count, cols):
                base = x0_rows[half, first:first + 1, cols]
                return bass.AP(tensor=base.tensor, offset=base.offset,
                               ap=[[CW, M], [STACK * CW, count], [1, cols.stop - cols.start]])

            def load(half, tiles, cols, loaded):
                for shift in range(STACK):
                    rows = slice(shift * M, (shift + 1) * M)
                    if tiles.start == 0:
                        sp.dma_start(plain[half][rows, cols], x0_rows[half, 0:M, cols]).then_inc(loaded, 16)
                    sp.dma_start(rotated[half][rows, tiles, cols],
                                 windows(half, STACK * tiles.start + shift, tiles.stop - tiles.start, cols)
                                 ).then_inc(loaded, 16)

            def rotate(c, half):
                sp.wait_ge(turn_copied, c + 1)
                for odd in range(2):
                    dims = x0_rows[half].rearrange("f (pair odd b) -> odd f pair b", odd=2, b=P)[odd]
                    own = x0_t[half][odd * M:(odd + 1) * M, :].rearrange("f (pair b) -> f pair b", b=P)
                    sp.dma_start(dims[0:M], own).then_inc(x0_sent, 16)
                    sp.dma_start(dims[M:WINDOW], own[0:WINDOW - M]).then_inc(x0_sent, 16)
                sp.wait_ge(x0_sent, (c + 1) * SENT)
                if is_first(c):
                    load(half, slice(0, FIRST_TILES), REST, first_in[0])
                    load(half, slice(FIRST_TILES, PAIR_TILES), REST, first_in[1])
                else:
                    load(half, slice(0, PAIR_TILES), slice(0, CW), rotated_in[half])

            for half in range(2):
                rotate(half, half)
            with sp.Fori(1, PAIRS) as pair:
                for half in range(2):
                    rotate(pair * 2 + half, half)
            for part, cols in enumerate((early, late)):
                sp.wait_ge(y_done, part + 1)
                sp.dma_start(out[cols, :].rearrange("b a -> a b"), y_row[0:1, cols]).then_inc(out_sent, 16)
            sp.wait_ge(out_sent, 2 * 16)

        @block.gpsimd
        def _(pool):
            def gather(tile, field):
                nc.gpsimd.indirect_dma_start(
                    out=gathered[:, field, tile * D:(tile + 1) * D], out_offset=None, in_=tables[field],
                    in_offset=bass.IndirectOffsetOnAxis(ap=idx_all[:, tile, field:field + 1], axis=0),
                ).then_inc(rows_in[tile], 16)

            def stage(c):
                pool.wait_ge(rows_in[c // CHUNKS_IN_TILE], 16 * M)
                after(pool, turned, c - 1)
                after(pool, x0_done, c - 1)
                nc.gpsimd.tensor_copy(staged[c % 2][:], gathered[:, :, c * CD:(c + 1) * CD].rearrange("p f d -> p d f")
                                      ).then_inc(x0_staged, 1)

            def sum_products(n, k):
                bank = prods[k % 2]
                total = sums[k % 2][:, POOL_SUMS:LAST_BANK, :].rearrange("p a s -> p (a s)")
                step = n * POOL_STEPS
                if n == LAST_TILE:
                    partial = [bank[:, 0], *(pool_sum[:, i] for i in range(3)), total]
                    after(pool, fold_step, n * 2 - 3)
                    for i in range(1, S_BANKS - 1):
                        pool.wait_ge(prods_done, n * S_BANKS + i + 1)
                        pool.wait_ge(pool_step, step + i - 1)
                        nc.gpsimd.tensor_tensor(partial[i], partial[i - 1], bank[:, i], ALU.add).then_inc(pool_step, 1)
                    return
                pool.wait_ge(prods_done, n * S_BANKS + 4)
                nc.gpsimd.tensor_tensor(pool_sum[:, 0:2], bank[:, 0:2], bank[:, 2:4], ALU.add).then_inc(pool_step, 1)
                pool.wait_ge(pool_step, step + 1)
                nc.gpsimd.tensor_tensor(pool_sum[:, 2], pool_sum[:, 0], pool_sum[:, 1], ALU.add).then_inc(pool_step, 1)
                pool.wait_ge(prods_done, n * S_BANKS + 5)
                pool.wait_ge(pool_step, step + 2)
                after(pool, fold_step, n * 2 - 3)
                nc.gpsimd.tensor_tensor(total, pool_sum[:, 2], bank[:, 4], ALU.add).then_inc(pool_step, 1)

            def early_sum(i):
                which, q = divmod(i, CHUNKS_IN_TILE - 1)
                of, to = ((p2_chunk, p2[:]), (p1_chunk, p1_t[:, early].rearrange("p (t s) -> p t s", s=P)))[which]
                parts = of[:, 0:EARLY_TILES * CHUNKS_IN_TILE * P].rearrange("p (t q s) -> p q t s", q=CHUNKS_IN_TILE, s=P)
                if q == 0:
                    pool.wait_ge(fold_step, EARLY_TILES * CHUNKS_IN_TILE * CD * 2)
                    pool.wait_ge(x1_used, EARLY_TILES * CHUNKS_IN_TILE * 2)
                else:
                    pool.wait_ge(early_summed, i)
                nc.gpsimd.tensor_tensor(to, parts[:, 0] if q == 0 else to, parts[:, q + 1], ALU.add).then_inc(early_summed, 1)

            def issued_by(n):
                if n < 0:
                    return M
                tile, at = divmod(n + D - LEAD, D)
                if tile == 0:
                    return M + EARLY + -(-(M - EARLY) * (at - D + LEAD + 1) // LEAD)
                return min(TILES * M, M * (tile + 1) + -(-M * (at + 1) // D))

            LEAD = 6
            EARLY = 16
            pool.wait_ge(ids_in, 16)
            for field in range(M):
                gather(0, field)
            stage(0)
            stage(1)
            issued = M
            for g in range(issued, issued + EARLY):
                gather(*divmod(g, M))
            issued += EARLY
            stage(2)
            for n in range(TILES * D):
                upto = issued_by(n)
                for g in range(issued, upto):
                    gather(*divmod(g, M))
                issued = upto
                sum_products(n, n % CD)
                if EARLY_SUMS_AT <= n < EARLY_SUMS_AT + EARLY_SUMS:
                    early_sum(n - EARLY_SUMS_AT)
                if n % CD == CD - 2 and n // CD + 3 < CHUNKS:
                    stage(n // CD + 3)

        @block.tensor
        def _(pe):
            def turn(c, half):
                pe.wait_ge(x0_staged, c + 1)
                after(pe, turn_copied, c)
                after(pe, x1_done, c * 2 - 2)
                for k in range(0, CD, 2):
                    last = nc.tensor.transpose(turn_bank[half][:, k // 2 * P:(k // 2 + 1) * P],
                                               staged[half][:, k:k + 2, :].rearrange("p d f -> p (d f)"), ident_f[:])
                last.then_inc(turned, 1)

            def contract_pairs(c, half, t, cols=slice(0, CW)):
                if t == 0 and not is_first(c) and exists(c + 1):
                    pe.wait_ge(turn_copied, c + 2)
                if t in SPLIT_TILES and not is_first(c):
                    i = SPLIT_TILES.index(t)
                    pe.wait_ge(pair_lo_done, (c - 1) * len(SPLIT_TILES) + (i + 1))
                    nc.tensor.matmul(x1_bank[:], w1_hi[:, i, :], pair_hi[i][:], start=False, stop=False)
                    nc.tensor.matmul(x1_bank[:], w1_lo[:, i, :], pair_hi[i][:], start=False, stop=False)
                    nc.tensor.matmul(x1_bank[:], w1_hi[:, i, :], pair_lo[i][:], start=False, stop=False).then_inc(pairs_done, 1)
                    return
                pe.wait_ge(product_done, products_by(c, t))
                rows = LAST_ROWS if t == PAIR_TILES - 1 else ROWS
                nc.tensor.matmul(x1_bank[:, cols], w1_sym[0:rows, t, :], rotated[half][0:rows, t, cols],
                                 start=(t == 0), stop=(t == PAIR_TILES - 1)).then_inc(pairs_done, 1)

            def rotate_first(bank, matrices):
                for place, t in enumerate(matrices):
                    last = nc.tensor.matmul(rotation_bank[bank][0:ROWS, place * P:(place + 1) * P],
                                            first_rotation[:, t, :], x0_t[0][0:M, 0:P], start=True, stop=True)
                last.then_inc(rotated_full, 1)

            def contract_first():
                pe.wait_ge(turn_copied, 2)
                order = [*LATER_MATRICES[:-1], *EARLIER_MATRICES]
                for i, t in enumerate(order):
                    pe.wait_ge(first_product_done, 1 if t in LATER_MATRICES else 2)
                    rows = LAST_ROWS if t == PAIR_TILES - 1 else ROWS
                    last = nc.tensor.matmul(x1_bank[:, 0:P], w1_sym[0:rows, t, :], first_pairs[0:rows, t, :],
                                            start=(i == 0), stop=(i == PAIR_TILES - 1))
                last.then_inc(first_pairs_done, 1)

            def first_layer_known(t, cols, bank):
                block = slice(t * P, (t + 1) * P)
                nc.tensor.matmul(bank[:, 0:cols.stop - cols.start], wt1[:, 0, block], p1_t[:, cols], start=True, stop=False)
                nc.tensor.matmul(bank[:, 0:cols.stop - cols.start], wt1_ctx[:, block], ctx_sb[:, cols], start=False, stop=False)

            def first_layer_p2(t, cols, bank):
                nc.tensor.matmul(bank[:, 0:cols.stop - cols.start], wt1[:, 1, t * P:(t + 1) * P], p2_t[:, cols],
                                 start=False, stop=True).then_inc(h1_full, 1)

            def second_layer(u, t, cols, bank):
                last = nc.tensor.matmul(bank[:, 0:cols.stop - cols.start], wt2[:, t, u * P:(u + 1) * P], h1[:, t, cols],
                                        start=(t == 0), stop=(t == T1 - 1))
                if t == T1 - 1:
                    last.then_inc(h2_full, 1)

            def third_layer(u, cols, bank):
                last = nc.tensor.matmul(bank[0:1, 0:cols.stop - cols.start], wt3[:, u:u + 1], h2[:, u, cols],
                                        start=(u == 0), stop=(u == T2 - 1))
                if u == T2 - 1:
                    last.then_inc(row_full, 1)

            def early_mlp(step):
                if step == TURN_STEP:
                    pe.wait_ge(early_summed, EARLY_SUMS // 2)
                    for b in range(EARLY_TILES):
                        last = nc.tensor.transpose(x1_bank[:, b * P:(b + 1) * P], p2[:, b, :], ident_f[:])
                    last.then_inc(p2_turned, 1)
                elif step < H2_STEP:
                    t = step - H1_STEP
                    if t == 0:
                        pe.wait_ge(top_in, 16 * TOP_DMAS)
                        pe.wait_ge(early_summed, EARLY_SUMS)
                        pe.wait_ge(p2_t_done, 1)
                    else:
                        pe.wait_ge(h1_done, t)
                    first_layer_known(t, early, x1_bank)
                    first_layer_p2(t, early, x1_bank)
                elif step < ROW_STEP:
                    u = step - H2_STEP
                    if u == 0:
                        pe.wait_ge(h1_done, T1)
                    else:
                        pe.wait_ge(h2_done, u)
                    for t in range(T1):
                        second_layer(u, t, early, x1_bank)
                else:
                    pe.wait_ge(h2_done, T2)
                    for u in range(T2):
                        third_layer(u, early, x1_bank)

            def chunk(c, half):
                if is_first(c):
                    pe.wait_ge(first_x1_done, 2)
                    pe.wait_ge(first_lo_done, 1)
                else:
                    pe.wait_ge(x1_done, c * 2 + 2)
                    pe.wait_ge(x1_used, c * 2 + 1)
                for slot in range(SLOTS):
                    if is_first(c) and slot == REST_PAIR_AT:
                        for t in range(PAIR_TILES):
                            contract_pairs(0, 0, t, REST)
                    if is_first(c) and slot == BANKS:
                        pe.wait_ge(x1_done, 2)
                        pe.wait_ge(x1_used, 1)
                    if not exists(c + 1) and slot in MLP_AT:
                        early_mlp(MLP_AT.index(slot))
                    if exists(c + 2) and slot == (TURN_AT_0 if is_first(c) else TURN_AT):
                        turn(c + 2, half)
                    pair_at = PAIR_AT_0 if is_first(c) else PAIR_AT
                    if exists(c + 1) and slot in pair_at:
                        contract_pairs(c + 1, 1 - half, pair_at.index(slot))
                    k, own = divmod(slot, BANKS)
                    first, width = fields_of(own)
                    cols = slice(first * S, (first + width) * S)
                    hi = x1_hi[half][:, k * P:(k + 1) * P]
                    lo = x1_lo[half][:, k * P:(k + 1) * P]
                    o = OWNER[own]
                    y = y_bank[o][nth(slot) % RING[o]][:, 0:width * S]
                    if o == "V":
                        after(pe, acc_done, c * ACCS + accs_before(nth(slot) - RING[o] + 1))
                    else:
                        after(pe, prods_done, c * (CD * S_BANKS) + (nth(slot) - RING[o] + 1))
                    nc.tensor.matmul(y, hi, w2_hi[:, cols], start=True, stop=False)
                    nc.tensor.matmul(y, hi, w2_lo[:, cols], start=False, stop=False)
                    nc.tensor.matmul(y, lo, w2_hi[:, cols], start=False, stop=True).then_inc(y_full[o], 1)

            pe.wait_ge(ident_in, 16)
            turn(0, 0)
            pe.wait_ge(rotation_in, 16)
            pe.wait_ge(turn_copied, 1)
            rotate_first(0, LATER_MATRICES)
            rotate_first(1, EARLIER_MATRICES)
            turn(1, 1)
            pe.wait_ge(w1_done, 1)
            contract_first()
            pe.wait_ge(w2_hi_done, 1)
            pe.wait_ge(w2_lo_done, 1)
            pe.wait_ge(w1_lo_done, 1)
            chunk_pairs(pe, chunk)

            pe.wait_ge(acc_done, CHUNKS * ACCS)
            pe.wait_ge(p1_done, 1)
            for t in range(T1):
                first_layer_known(t, late, h1_bank[t])
            pe.wait_ge(fold_step, CHUNKS * CD * 2)
            pe.wait_ge(prods_done, CHUNKS * CD * S_BANKS)
            nc.tensor.transpose(p2_bank[:, 0:P], p2_chunk[:, (CHUNKS - 1) * S:CHUNKS * S], ident_f[:]).then_inc(p2_turned, 1)
            pe.wait_ge(p2_t_done, 2)
            for t in range(T1):
                first_layer_p2(t, late, h1_bank[t])
            for t in range(T1):
                pe.wait_ge(h1_done, T1 + t + 1)
                for u in range(T2):
                    second_layer(u, t, late, h2_bank[u])
            pe.wait_ge(y_done, 1)
            for u in range(T2):
                pe.wait_ge(h2_done, T2 + u + 1)
                third_layer(u, late, x1_bank)

        @block.scalar
        def _(act):
            def scalars(c, half):
                act.wait_ge(x0_staged, c + 1)
                after(act, acc_done, (c - 1) * ACCS)
                after(act, prods_done, (c - 1) * (CD * S_BANKS))
                nc.scalar.activation(x0_chunk[half][:], staged[half][:], ACT.Copy).then_inc(x0_done, 1)

            def pair_high(c, half, i):
                t = SPLIT_TILES[i]
                act.wait_ge(product_done, products_by(c, t))
                after(act, pairs_done, (c - 1) * PAIR_TILES + (t + 1))
                nc.scalar.activation(pair_hi[i][:], rotated[half][:, t, :], ACT.Copy).then_inc(pair_hi_done, 1)

            def copy_turned(c, half):
                act.wait_ge(turned, c + 1)
                after(act, x0_sent, (c - 1) * SENT)
                nc.scalar.activation(x0_t[half][:], turn_bank[half], ACT.Copy).then_inc(turn_copied, 1)

            def relu_x1(half, cols, done):
                nc.scalar.activation(x1[:, cols], x1_bank[:, cols], ACT.Relu, bias=b1_col[:]).then_inc(done, 1)
                nc.scalar.activation(x1_hi[half][:, cols], x1_bank[:, cols], ACT.Relu, bias=b1_col[:]).then_inc(done, 1)

            def finish_x1(c, half, cols=slice(0, CW)):
                act.wait_ge(pairs_done, (c + 1) * PAIR_TILES)
                after(act, x1_used, c * 2)
                relu_x1(half, cols, x1_done)

            def finish_h1(t, part, cols, bank):
                act.wait_ge(h1_full, part * T1 + t + 1)
                nc.scalar.activation(h1[:, t, cols], bank[:, 0:cols.stop - cols.start], ACT.Relu,
                                     bias=bt1[:, t:t + 1]).then_inc(h1_done, 1)

            def finish_h2(u, part, cols, bank):
                act.wait_ge(h2_full, part * T2 + u + 1)
                nc.scalar.activation(h2[:, u, cols], bank[:, 0:cols.stop - cols.start], ACT.Relu,
                                     bias=bt2[:, u:u + 1]).then_inc(h2_done, 1)

            def chunk(c, half):
                act.wait_ge(x0_done, c + 1)
                for slot in range(SLOTS):
                    if not exists(c + 1) and slot in MLP_READ_AT:
                        step = MLP_READ_AT.index(slot)
                        if step == H1_STEP:
                            act.wait_ge(top_in, 16 * TOP_DMAS)
                        if H1_STEP <= step < H2_STEP:
                            finish_h1(step - H1_STEP, 0, early, x1_bank)
                        if H2_STEP <= step < ROW_STEP:
                            finish_h2(step - H2_STEP, 0, early, x1_bank)
                    if is_first(c) and slot == REST_COPY_AT:
                        finish_x1(0, 0, REST)
                    if exists(c + 2) and slot == (TURN_COPY_AT_0 if is_first(c) else TURN_COPY_AT):
                        copy_turned(c + 2, half)
                    if exists(c + 1):
                        hi_at = PAIR_HI_AT_0 if is_first(c) else PAIR_HI_AT
                        if slot in hi_at:
                            pair_high(c + 1, 1 - half, hi_at.index(slot))
                        if slot == SCALARS_AT:
                            scalars(c + 1, 1 - half)
                        if slot == X1_COPY_AT:
                            finish_x1(c + 1, 1 - half)
                    k, own = divmod(slot, BANKS)
                    if OWNER[own] != "S":
                        continue
                    first, width = fields_of(own)
                    bank = OWNER[:own].count("S")
                    act.wait_ge(y_full["S"], c * (CD * S_BANKS) + (nth(slot) + 1))
                    if bank == 0:
                        after(act, pool_step, (c * CD + (k - 1)) * POOL_STEPS)
                    if bank < S_BANKS - 1:
                        to = prods[k % 2][:, bank]
                    else:
                        after(act, fold_step, (c * CD + k) * 2 - 3)
                        to = sums[k % 2][:, LAST_BANK:SUMS, :].rearrange("p a s -> p (a s)")
                    for f in range(width):
                        last = nc.scalar.activation(
                            to[:, f * S:(f + 1) * S], y_bank["S"][nth(slot) % RING["S"]][:, f * S:(f + 1) * S],
                            ACT.Copy, scale=x0_chunk[half][:, k, first + f:first + f + 1])
                    last.then_inc(prods_done, 1)

            act.wait_ge(w2_in, 16)
            nc.scalar.activation(w2_hi[:], w2_f[:], ACT.Copy).then_inc(w2_hi_done, 1)
            act.wait_ge(w1_done, 1)
            nc.scalar.activation(w1_hi[:], w1_sym[:, SPLIT, :], ACT.Copy).then_inc(w1_hi_done, 1)
            copy_turned(0, 0)
            act.wait_ge(rotated_full, 1)
            nc.scalar.activation(first_plain, rotation_bank[0][0:ROWS, (FIELDS_IN_BANK - 1) * P:], ACT.Copy
                                 ).then_inc(first_plain_done, 1)
            copy_turned(1, 1)
            scalars(0, 0)
            act.wait_ge(first_pairs_done, 1)
            relu_x1(0, slice(0, P), first_x1_done)
            chunk_pairs(act, chunk)

            for t in range(T1):
                finish_h1(t, 1, late, h1_bank[t])
            for u in range(T2):
                finish_h2(u, 1, late, h2_bank[u])

        @block.vector
        def _(dve):
            def multiply_first(bank, tiles):
                dve.wait_ge(rotated_full, bank + 1)
                plain_rows = first_plain.rearrange("p (a b) -> p a b", a=1).broadcast_to([ROWS, len(tiles), P])
                nc.vector.tensor_tensor(
                    first_pairs[:, tiles[0]:tiles[-1] + 1, :],
                    rotation_bank[bank][0:ROWS, 0:len(tiles) * P].rearrange("p (a b) -> p a b", b=P),
                    plain_rows, ALU.mult).then_inc(first_product_done, 1)

            def multiply_pairs(c, half, t, cols=slice(0, CW)):
                if is_first(c):
                    dve.wait_ge(first_in[0], 16 * 2 * STACK)
                    if t >= FIRST_TILES:
                        dve.wait_ge(first_in[1], 16 * STACK)
                else:
                    dve.wait_ge(rotated_in[half], (c + half) * (16 * STACK))
                pairs = rotated[half][:, t, cols]
                nc.vector.tensor_tensor(pairs, pairs, plain[half][:, cols], ALU.mult).then_inc(product_done, 1)

            def pair_low(c, half, i):
                t = SPLIT_TILES[i]
                dve.wait_ge(pair_hi_done, (c - 1) * len(SPLIT_TILES) + (i + 1))
                nc.vector.tensor_tensor(pair_lo[i][:], rotated[half][:, t, :], pair_hi[i][:].bitcast(F32),
                                        ALU.subtract).then_inc(pair_lo_done, 1)

            def split_x1(half, cols, done):
                nc.vector.tensor_tensor(x1_lo[half][:, cols], x1[:, cols], x1_hi[half][:, cols].bitcast(F32),
                                        ALU.subtract).then_inc(done, 1)

            def sum_x1(c):
                nc.vector.tensor_reduce(p1_chunk[:, bass.ds(c * P, P)], x1[:].rearrange("h (d b) -> h b d", d=CD),
                                        AX.X, ALU.add).then_inc(x1_used, 1)

            def fold(c, k):
                n = c * CD + k
                here = p2_chunk[:, bass.ds(c * S, S)]
                dve.wait_ge(pool_step, (n + 1) * POOL_STEPS if not is_last(n) else n * POOL_STEPS + S_BANKS - 2)
                dve.wait_ge(prods_done, n * S_BANKS + S_BANKS)
                dve.wait_ge(acc_done, c * ACCS + (k + 1) * TILE_ACCS)
                nc.vector.tensor_reduce(x2[:, k % 2, :], sums[k % 2][:].rearrange("p a s -> p s a"),
                                        AX.X, ALU.add).then_inc(fold_step, 1)
                dve.wait_ge(fold_step, n * 2 + 1)
                if k == 0 and not exists(c + 1):
                    dve.wait_ge(p2_done, 1)
                if k == 0 and exists(c + 1):
                    nc.vector.tensor_scalar(here, x2[:, k % 2, :], 0.0, None, ALU.max).then_inc(fold_step, 1)
                else:
                    nc.vector.scalar_tensor_tensor(out=here, in0=x2[:, k % 2, :], scalar=0.0, in1=here,
                                                   op0=ALU.max, op1=ALU.add).then_inc(fold_step, 1)

            def sum_chunks(to, of, chunks):
                first = EARLY_TILES * CHUNKS_IN_TILE * P
                return nc.vector.tensor_reduce(to, of[:, first:first + chunks * P].rearrange("p (q s) -> p s q", s=P),
                                               AX.X, ALU.add)

            def chunk(c, half):
                dve.wait_ge(x0_done, c + 1)
                for slot in range(SLOTS):
                    if not exists(c + 1):
                        if slot == P1_AT:
                            dve.wait_ge(x1_used, CHUNKS * 2)
                            sum_chunks(p1_t[:, late], p1_chunk, CHUNKS_IN_TILE).then_inc(p1_done, 1)
                        if slot == MLP_READ_AT[TURN_STEP]:
                            dve.wait_ge(p2_turned, 1)
                            nc.vector.tensor_copy(p2_t[:, early], x1_bank[:, early]).then_inc(p2_t_done, 1)
                        if slot == MLP_READ_AT[ROW_STEP]:
                            dve.wait_ge(row_full, 1)
                            nc.vector.tensor_copy(y_row[0:1, early], x1_bank[0:1, early]).then_inc(y_done, 1)
                    if is_first(c):
                        if slot == REST_PRODUCT_AT:
                            for t in range(PAIR_TILES):
                                multiply_pairs(0, 0, t, REST)
                        if slot == REST_SPLIT_AT:
                            dve.wait_ge(x1_done, 2)
                            split_x1(0, REST, x1_used)
                        if slot == REST_SUM_AT:
                            sum_x1(0)
                    if exists(c + 1):
                        product_at = PRODUCT_AT_0 if is_first(c) else PRODUCT_AT
                        if slot in product_at:
                            multiply_pairs(c + 1, 1 - half, product_at.index(slot))
                        lo_at = PAIR_LO_AT_0 if is_first(c) else PAIR_LO_AT
                        if slot in lo_at:
                            pair_low(c + 1, 1 - half, lo_at.index(slot))
                        if slot == X1_SPLIT_AT:
                            dve.wait_ge(x1_done, (c + 1) * 2 + 2)
                            split_x1(1 - half, slice(0, CW), x1_used)
                        if slot == X1_SUM_AT:
                            sum_x1(c + 1)
                    k, own = divmod(slot, BANKS)
                    if own == FOLD_AT:
                        if k > 0:
                            fold(c, k - 1)
                        elif not (isinstance(c, int) and c == 0):
                            fold(c - 1, CD - 1)
                            if not exists(c + 1):
                                dve.wait_ge(fold_step, c * CD * 2)
                                sum_chunks(p2_chunk[:, c * S:(c + 1) * S], p2_chunk, CHUNKS_IN_TILE - 1).then_inc(p2_done, 1)
                    if OWNER[own] != "V":
                        continue
                    first, width = fields_of(own)
                    dve.wait_ge(y_full["V"], c * (CD * V_BANKS) + (nth(slot) + 1))
                    for f in range(width):
                        step = accs_before(nth(slot)) + f
                        y = y_bank["V"][nth(slot) % RING["V"]][:, f * S:(f + 1) * S]
                        x = x0_chunk[half][:, k, first + f:first + f + 1]
                        acc = sums[k % 2][:, (step - k * TILE_ACCS) % 2, :]
                        after(dve, acc_done, c * ACCS + (step - 1))
                        if own == 0 and f == 0:
                            after(dve, fold_step, (c * CD + k) * 2 - 3)
                        if own == 0 and f == 1:
                            nc.vector.tensor_scalar(acc, y, x, None, ALU.mult).then_inc(acc_done, 1)
                        else:
                            start = own == 0 and f == 0
                            nc.vector.scalar_tensor_tensor(out=acc, in0=y, scalar=x, in1=b2_rows[:] if start else acc,
                                                           op0=ALU.mult, op1=ALU.add).then_inc(acc_done, 1)

            dve.wait_ge(w1_in, 48)
            nc.vector.memset(w1_other[0:M, 0, :], 0.0).then_inc(w1_zeroed, 1)
            dve.wait_ge(w1_zeroed, 1)
            nc.vector.tensor_tensor(w1_sym[:], w1_sym[:], w1_other[:], ALU.add).then_inc(w1_done, 1)
            dve.wait_ge(w1_hi_done, 1)
            nc.vector.tensor_tensor(w1_lo[:], w1_sym[:, SPLIT, :], w1_hi[:].bitcast(F32), ALU.subtract).then_inc(w1_lo_done, 1)
            dve.wait_ge(w2_hi_done, 1)
            nc.vector.tensor_tensor(w2_lo[:], w2_f[:], w2_hi[:].bitcast(F32), ALU.subtract).then_inc(w2_lo_done, 1)
            dve.wait_ge(first_plain_done, 1)
            multiply_first(0, LATER_MATRICES[:-1])
            multiply_first(1, EARLIER_MATRICES)
            dve.wait_ge(first_x1_done, 2)
            split_x1(0, slice(0, P), first_lo_done)
            dve.wait_ge(b2_in, 16)
            chunk_pairs(dve, chunk)

            fold(CHUNKS - 1, CD - 1)
            dve.wait_ge(p2_turned, 2)
            nc.vector.tensor_copy(p2_t[:, late], p2_bank[:, 0:P]).then_inc(p2_t_done, 1)
            dve.wait_ge(row_full, 2)
            nc.vector.tensor_copy(y_row[0:1, late], x1_bank[0:1, 0:P]).then_inc(y_done, 1)


def kernel(**inputs):
    import numpy as np
    import concourse.bacc as bacc
    from concourse.bass_utils import run_bass_kernel_spmd

    nc = bacc.Bacc("TRN2", target_bir_lowering=False, num_devices=1)
    arrays = {}

    def dram(name, array):
        array = np.ascontiguousarray(array)
        arrays[name] = array
        return nc.dram_tensor(name, array.shape, mybir.dt.from_np(array.dtype), kind="ExternalInput").ap()

    jj, h = np.divmod(np.arange(ROWS), M)
    shift = STACK * np.arange(PAIR_TILES)[None, :] + jj[:, None]
    here = np.broadcast_to(h[:, None], shift.shape)
    there = (here + shift) % M
    fields = np.concatenate([there, here[:, 0:1]], axis=1)
    rotation = (np.arange(M)[:, None, None] == fields.T[None]).astype(np.float32)
    w1 = np.transpose(np.asarray(inputs["L0_rec_W1"]), (1, 2, 0))
    w2 = np.transpose(np.asarray(inputs["L0_rec_W2"]), (1, 2, 0)).reshape(S, M * S)
    def columns(name):
        return np.asarray(inputs[name]).reshape(-1, P).T

    table_names = [f"tbl_{f}" for f in range(M)]
    args = dict(
        ids=dram("ids", inputs["ids"]),
        tables=[dram(n, inputs[n]) for n in table_names],
        ctx_t=dram("ctx_t", np.transpose(np.asarray(inputs["dense_ctx"]))),
        w1_a=dram("w1_a", w1[here, there]), w1_b=dram("w1_b", w1[there, here]),
        rotation=dram("rotation", rotation),
        b1=dram("b1", inputs["L0_rec_b1"]), w2_t=dram("w2_t", w2), b2=dram("b2", inputs["L0_rec_b2"]),
        ident=dram("ident", np.eye(P, dtype=np.float32)),
        w_top1=dram("w_top1", inputs["W_top1"]), b_top1=dram("b_top1", columns("b_top1")),
        w_top2=dram("w_top2", inputs["W_top2"]), b_top2=dram("b_top2", columns("b_top2")),
        w_top3=dram("w_top3", columns("W_top3")),
    )
    out = nc.dram_tensor("out", (inputs["ids"].shape[0], 1), F32, kind="ExternalOutput").ap()
    x0_rows = nc.dram_tensor("x0_rows", (2, WINDOW, CW), F32).ap()
    build(nc, x0_rows=x0_rows, out=out, **args)
    r = run_bass_kernel_spmd(nc, [arrays], core_ids=[0])
    return r.results[0]["out"]
```
